# Optimizing a Trainium2 kernel written in Bass

```python
import numpy as np
import jax
import jax.numpy as jnp

def _softmax(x, axis=-1):
    return jax.nn.softmax(x, axis=axis)

def _gelu(x):
    return jax.nn.gelu(x, approximate=True)

def _silu(x):
    return jax.nn.silu(x)

def _sigmoid(x):
    return jax.nn.sigmoid(x)

def _layernorm(x, axis=-1, eps=1e-05):
    m = jnp.mean(x, axis=axis, keepdims=True)
    v = jnp.var(x, axis=axis, keepdims=True)
    return (x - m) / jnp.sqrt(v + eps)

def _scatter_add(tgt, idx, src, axis=0):
    return tgt.at[idx].add(src)

def _segment_sum(src, seg, n):
    return jax.ops.segment_sum(src, seg, n)
kernel_name = 'mk_adj_ffn_d1_adj_r2_ef4ee1'

def setup_inputs(seed: int=0):
    np.random.seed(seed)
    _w = jnp.asarray

    def _rec_inputs():
        import jax
        import jax.numpy as jnp
        _gk = jax.random.key(seed)
        x = -0.0005207 + 1.001 * jax.random.normal(jax.random.fold_in(_gk, 1), (3327, 128), jnp.float32)
        _a = jax.random.bernoulli(jax.random.fold_in(_gk, 2), 0.00120228, (3327, 3327))
        adj = _a.astype(jnp.int32)
        return (x, adj)
    x, adj = _rec_inputs()

    def _L0_gnn_setup():
        import jax, jax.numpy as jnp
        import numpy as np
        N, D, H = (4096, 128, 128)
        KEEP_RATIO = 0.5
        TEMP = 1.0
        COS_EPS = 0.0001
        NEG = -9000000000000000.0

        def _cos_normalize(x):
            n = jnp.linalg.norm(x, axis=-1, keepdims=True)
            return x / jnp.maximum(n, COS_EPS)
        key = jax.random.key(seed)
        k1, k2, k3, k4 = jax.random.split(key, 4)
        features = jax.random.normal(k1, (N, D), dtype=jnp.float32)
        adj = jax.random.randint(k2, (N, N), 0, 2, dtype=jnp.int32)
        Wq = jax.random.normal(k3, (H, D), dtype=jnp.float32) * 0.001
        Wk = jax.random.normal(k4, (H, D), dtype=jnp.float32) * 0.001
        return {'features': features, 'adj': adj, 'Wq': Wq, 'Wk': Wk}
    _L0_gnn_all = _L0_gnn_setup()
    _L0_gnn_in = {k: v for k, v in _L0_gnn_all.items() if k in ('Wq', 'Wk')}
    del _L0_gnn_all

    def _L0_ffn_setup():
        import jax, jax.numpy as jnp
        import numpy as np
        B, T, C = (64, 192, 128)
        NH, NKV = (4, 2)
        HD = C // NH
        NREP = NH // NKV
        NE, TOPK = (8, 2)
        HID = int(8 / 3 * C)
        EPS_RMS = 1e-06

        def _rope_tables(t_len):
            inv_freq = 1.0 / 10000.0 ** (np.arange(0, HD, 2, dtype=np.float32) / HD)
            t = np.arange(t_len, dtype=np.float32)
            freqs = np.outer(t, inv_freq)
            emb = np.concatenate([freqs, freqs], axis=-1)
            return (jnp.asarray(np.cos(emb)), jnp.asarray(np.sin(emb)))

        def _rotate_half(x):
            h = x.shape[-1] // 2
            return jnp.concatenate([-x[..., h:], x[..., :h]], axis=-1)

        def _rmsnorm(v, w):
            return v * jax.lax.rsqrt(jnp.mean(v * v, axis=-1, keepdims=True) + EPS_RMS) * w
        key = jax.random.key(seed)
        ks = jax.random.split(key, 10)
        s = lambda k, shape: jax.random.normal(k, shape, jnp.float32) * 0.02
        return {'x': jax.random.normal(ks[0], (B, T, C), jnp.float32), 'ln1_w': jnp.ones((C,), jnp.float32), 'ln2_w': jnp.ones((C,), jnp.float32), 'wq': s(ks[1], (NH * HD, C)), 'wk': s(ks[2], (NKV * HD, C)), 'wv': s(ks[3], (NKV * HD, C)), 'wo': s(ks[4], (C, C)), 'router_w': s(ks[5], (NE, C)), 'w1': s(ks[6], (NE, HID, C)), 'w2': s(ks[7], (NE, C, HID)), 'w3': s(ks[8], (NE, HID, C))}
    _L0_ffn_all = _L0_ffn_setup()
    _L0_ffn_in = {k: v for k, v in _L0_ffn_all.items() if k in ('ln1_w', 'ln2_w', 'wq', 'wk', 'wv', 'wo', 'router_w', 'w1', 'w2', 'w3')}
    del _L0_ffn_all
    return {'x': x, 'adj': adj, 'L0_gnn_Wq': _L0_gnn_in['Wq'], 'L0_gnn_Wk': _L0_gnn_in['Wk'], 'L0_ffn_ln1_w': _L0_ffn_in['ln1_w'], 'L0_ffn_ln2_w': _L0_ffn_in['ln2_w'], 'L0_ffn_wq': _L0_ffn_in['wq'], 'L0_ffn_wk': _L0_ffn_in['wk'], 'L0_ffn_wv': _L0_ffn_in['wv'], 'L0_ffn_wo': _L0_ffn_in['wo'], 'L0_ffn_router_w': _L0_ffn_in['router_w'], 'L0_ffn_w1': _L0_ffn_in['w1'], 'L0_ffn_w2': _L0_ffn_in['w2'], 'L0_ffn_w3': _L0_ffn_in['w3']}

def reference(x, adj, L0_gnn_Wq, L0_gnn_Wk, L0_ffn_ln1_w, L0_ffn_ln2_w, L0_ffn_wq, L0_ffn_wk, L0_ffn_wv, L0_ffn_wo, L0_ffn_router_w, L0_ffn_w1, L0_ffn_w2, L0_ffn_w3):
    import jax
    import jax.numpy as jnp

    def _L0_gnn_ref(features, adj, Wq, Wk):
        import jax, jax.numpy as jnp
        import numpy as np
        N, D, H = (4096, 128, 128)
        KEEP_RATIO = 0.5
        TEMP = 1.0
        COS_EPS = 0.0001
        NEG = -9000000000000000.0

        def _cos_normalize(x):
            n = jnp.linalg.norm(x, axis=-1, keepdims=True)
            return x / jnp.maximum(n, COS_EPS)
        Qn = _cos_normalize(features @ Wq.T)
        Kn = _cos_normalize(features @ Wk.T)
        raw_att = Kn @ Qn.T
        att = jnp.where(adj > 0, raw_att, NEG) * TEMP
        att = jax.nn.softmax(att, axis=1)
        prop_fea = att @ features
        adj_mask = (jnp.sum(adj, axis=1) > 0).astype(features.dtype)[:, None]
        prop_fea = adj_mask * prop_fea + (1.0 - adj_mask) * features
        return (1.0 - KEEP_RATIO) * prop_fea + KEEP_RATIO * features

    def _L0_ffn_ref(x, ln1_w, ln2_w, wq, wk, wv, wo, router_w, w1, w2, w3):
        import jax, jax.numpy as jnp
        import numpy as np
        B, T, C = (64, 192, 128)
        NH, NKV = (4, 2)
        HD = C // NH
        NREP = NH // NKV
        NE, TOPK = (8, 2)
        HID = int(8 / 3 * C)
        EPS_RMS = 1e-06

        def _rope_tables(t_len):
            inv_freq = 1.0 / 10000.0 ** (np.arange(0, HD, 2, dtype=np.float32) / HD)
            t = np.arange(t_len, dtype=np.float32)
            freqs = np.outer(t, inv_freq)
            emb = np.concatenate([freqs, freqs], axis=-1)
            return (jnp.asarray(np.cos(emb)), jnp.asarray(np.sin(emb)))

        def _rotate_half(x):
            h = x.shape[-1] // 2
            return jnp.concatenate([-x[..., h:], x[..., :h]], axis=-1)

        def _rmsnorm(v, w):
            return v * jax.lax.rsqrt(jnp.mean(v * v, axis=-1, keepdims=True) + EPS_RMS) * w
        Bx, Tx, Cx = x.shape
        h = _rmsnorm(x, ln1_w)
        q = (h @ wq.T).reshape(Bx, Tx, NH, HD).transpose(0, 2, 1, 3)
        k = (h @ wk.T).reshape(Bx, Tx, NKV, HD).transpose(0, 2, 1, 3)
        v = (h @ wv.T).reshape(Bx, Tx, NKV, HD).transpose(0, 2, 1, 3)
        cos, sin = _rope_tables(Tx)
        cos, sin = (cos[None, None], sin[None, None])
        q = q * cos + _rotate_half(q) * sin
        k = k * cos + _rotate_half(k) * sin
        k = jnp.repeat(k, NREP, axis=1)
        v = jnp.repeat(v, NREP, axis=1)
        scores = jnp.einsum('bhtd,bhsd->bhts', q, k) / jnp.sqrt(jnp.float32(HD))
        causal = jnp.tril(jnp.ones((Tx, Tx), dtype=bool))
        scores = jnp.where(causal[None, None], scores, jnp.float32(-1e+30))
        att = jax.nn.softmax(scores, axis=-1)
        y = jnp.einsum('bhts,bhsd->bhtd', att, v).transpose(0, 2, 1, 3).reshape(Bx, Tx, Cx)
        x = x + y @ wo.T
        flat = _rmsnorm(x, ln2_w).reshape(-1, Cx)
        probs = jax.nn.softmax(flat @ router_w.T, axis=-1)
        tp, ti = jax.lax.top_k(probs, TOPK)
        tp = tp / (jnp.sum(tp, axis=-1, keepdims=True) + 1e-09)
        weights = jnp.sum(tp[..., None] * jax.nn.one_hot(ti, NE, dtype=flat.dtype), axis=1)
        out = jnp.zeros_like(flat)
        for e in range(NE):
            hh = jax.nn.silu(flat @ w1[e].T) * (flat @ w3[e].T)
            out = out + weights[:, e:e + 1] * (hh @ w2[e].T)
        return x + out.reshape(Bx, Tx, Cx)
    x = x + _L0_gnn_ref(_layernorm(x, axis=-1), adj, L0_gnn_Wq, L0_gnn_Wk)
    x = x + _L0_ffn_ref(_layernorm(x, axis=-1)[None], L0_ffn_ln1_w, L0_ffn_ln2_w, L0_ffn_wq, L0_ffn_wk, L0_ffn_wv, L0_ffn_wo, L0_ffn_router_w, L0_ffn_w1, L0_ffn_w2, L0_ffn_w3)[0]
    return x

_drawn_inputs = setup_inputs


def setup_inputs(seed=0):
    import zlib

    import numpy as np

    out = dict(_drawn_inputs(seed))
    spreads = {'L0_ffn_ln1_w': (1.0, 0.6), 'L0_ffn_ln2_w': (1.0, 0.6)}
    factors = {'L0_gnn_Wq': 4.779,
     'L0_gnn_Wk': 4.739,
     'L0_ffn_wq': 8.0,
     'L0_ffn_wk': 8.0,
     'L0_ffn_wv': 8.0,
     'L0_ffn_wo': 8.0,
     'L0_ffn_router_w': 8.0,
     'L0_ffn_w1': 8.0,
     'L0_ffn_w2': 8.0,
     'L0_ffn_w3': 8.0}
    for name, (base, spread) in spreads.items():
        noise = np.random.default_rng([zlib.crc32(name.encode()), seed]).standard_normal(out[name].shape)
        drawn = base * np.exp(spread * noise) if base else spread * noise
        out[name] = jnp.asarray(drawn.astype(out[name].dtype))
    for name, factor in factors.items():
        out[name] = (out[name] * factor).astype(out[name].dtype)
    return out
```

```python
from contextlib import ExitStack

import numpy as np

import concourse.bass as bass
from concourse import mybir

F32 = mybir.dt.float32
F16 = mybir.dt.float16
I32 = mybir.dt.int32
ALU = mybir.AluOpType
ACT = mybir.ActivationFunctionType
X = mybir.AxisListType.X

P = 128
NTOK = 3327
C = 128
NT = -(-NTOK // P)
NB = NT // 2
BT = 2 * P
TP = NT * P
NH, NKV, HD = 4, 2, 32
VW = 2 * HD + 1
NE = 8
HID = int(8 / 3 * C)
HC = -(-HID // P)
HW = HC * P
LN_EPS = 1e-5
RMS_EPS = 1e-6
COS_EPS = 1e-4
UNIT = 64.0
SCALE = float(HD) ** -0.5
FAR = -60000.0
LOWEST = -3.0e38


class Count:

    def __init__(self, eng, name, start):
        self.eng = eng
        self.reg = eng.alloc_register(name)
        eng.reg_mov(self.reg, start)

    def up(self, by=1):
        self.eng.reg_add(self.reg, self.reg, by)

    def now(self):
        return self.reg


def wait(eng, sem, value):
    if isinstance(value, int) and value <= 0:
        return
    eng.wait_ge(sem, value)


def skewed(eng, n, stages):
    most = max(lag for lag, _ in stages)
    lead = most + 2
    for k in range(lead):
        for lag, stage in stages:
            if k >= lag:
                stage(k - lag)
    with eng.Fori(lead, n) as k:
        for lag, stage in stages:
            stage(k - lag)
    for k in range(n, n + most):
        for lag, stage in stages:
            if k - lag < n:
                stage(k - lag)


def graph_ffn_program(nc, x, adj, w_small, w1, w3, w2, rope, tables, tables16, out):
    ctx = ExitStack()
    with ctx:
        def sb(name, shape, dt):
            return ctx.enter_context(nc.sbuf_tensor(name, shape, dt))

        def sem(name):
            return ctx.enter_context(nc.semaphore(name))

        X1 = sb("X1", [P, NT, C], F32)
        H1 = sb("H1", [P, NT, C + 1], F32)
        U = sb("U", [P, NT, C], F32)
        adj_bytes = sb("adj_bytes", [P, 2 * NT * BT], I32)
        half_bytes = sb("half_bytes", [P, 4 * TP], F16)
        Qs = sb("Qs", [P, NB, NH, BT], F16)
        Ks = sb("Ks", [P, NKV, TP], F16)
        V16 = sb("V16", [P, NT, NKV, VW], F16)
        adj2 = adj_bytes[:, :].rearrange("p (s t c) -> p s t c", s=2, t=NT)
        rope_f = adj_bytes[:, 0:2 * TP].bitcast(F32).rearrange("p (a t) -> p a t", a=2)
        moe_bytes = adj_bytes[:, :].bitcast(F16)
        ew = NE * HW
        W1h, W1l, W3h, W3l = (moe_bytes[:, k * ew:(k + 1) * ew] for k in range(4))
        F16h = moe_bytes[:, 4 * ew:4 * ew + TP]
        F16l = moe_bytes[:, 4 * ew + TP:4 * ew + 2 * TP]
        w2_at = (4 * ew + 2 * TP) // 2
        W2 = adj_bytes[:, w2_at:w2_at + NE * HC * C].bitcast(F32)
        QKh = half_bytes[:, 0:2 * TP].rearrange("p (a t) -> p a t", a=2)
        QKl = half_bytes[:, 2 * TP:4 * TP].rearrange("p (a t) -> p a t", a=2)
        W1f = half_bytes[:, 0:2 * ew].bitcast(F32)
        W3f = half_bytes[:, 2 * ew:4 * ew].bitcast(F32)
        SQ = Ks[:, :, :].rearrange("p a t -> p (a t)").bitcast(F32).rearrange("p (t c) -> p t c", c=C)

        small = sb("small", [P, w_small.shape[1]], F32)
        at = 0
        def cut(n, rows=P):
            nonlocal at
            at += n
            return small[0:rows, at - n:at]
        Wqk = cut(2 * C)
        Wf = cut(4 * P)
        Wv = cut(NKV * HD)
        Wr = cut(NE)
        WoA = cut(NH * (C + 1), VW).rearrange("p (h c) -> p h c", h=NH)
        ln1 = cut(1)
        ln2 = cut(1)
        tab = sb("tab", [P, tables.shape[1]], F32)
        ident = tab[:, 0:P]
        ones = tab[:, P:2 * P]
        negblk = tab[0:NH, 2 * P:2 * P + NH * P].rearrange("p (h t) -> p h t", h=NH)
        rev = tab[:, 2 * P + NH * P:2 * P + NH * P + NE]
        tab16 = sb("tab16", [P, tables16.shape[1]], F16)
        ident16 = tab16[:, 0:P]
        maskA = tab16[:, P:P + 1024].rearrange("p (t c) -> p t c", t=2)
        maskB = tab16[:, P + 1024:P + 2048].rearrange("p (t c) -> p t c", t=2)
        zero16 = sb("zero16", [P, 512], F16)

        stat = sb("stat", [P, 4, NT], F32)
        bias = sb("bias", [P, 2], F32)
        nb_ = sb("nb", [P, 2, C], F32)
        tb = sb("tb", [P, BT], F32)
        tmp = sb("tmp", [P, 4096], F32)
        sq, nrm, qn = tmp[:, 0:512], tmp[:, 512:1024], tmp[:, 1024:1536]
        Eg = [tmp[:, 1536 + 256 * k:1792 + 256 * k] for k in range(2)]
        Em = [tmp[:, 2048 + 256 * k:2304 + 256 * k] for k in range(2)]
        ra, rb, qr = tmp[:, 2560:3072], tmp[:, 3072:3584], tmp[:, 3584:4096]
        E = [tmp[:, 1024 * k:1024 * k + 1024] for k in range(2)]
        Eh = [tmp[:, 2048 + 512 * k:2560 + 512 * k].bitcast(F16) for k in range(2)]
        El = [tmp[:, 3072 + 512 * k:3584 + 512 * k].bitcast(F16) for k in range(2)]
        sl = [tmp[:, 768 * k:768 * k + 768] for k in range(2)]
        hh_ = [tmp[:, 1536 + 768 * k:2304 + 768 * k] for k in range(2)]
        gs = sb("gs", [P, 8], F32)
        gt = sb("gt", [P, 2, C], F32)
        OT = sb("OT", [P, NKV, 512], F32)
        cm = sb("cm", [P, 2, NH, NB], F32)
        m8 = sb("m8", [P, 2, NH], F32)
        zr = sb("zr", [P, 2], F32)
        LG = sb("LG", [P, NT, NE], F32)
        R = [sb(f"R{k}", [P, NT, NE], F32) for k in range(4)]
        GW = sb("GW", [P, NT, NE], F32)
        rs = sb("rs", [P, 6, NT], F32)

        ps = ctx.enter_context(nc.psum_tensor("ps", [P, 8, 512], F32))

        x_in, small_in, tab_in, rope_in, w_in, w2_in = map(sem, (
            "x_in", "small_in", "tab_in", "rope_in", "w_in", "w2_in"))
        adj_in = [sem("adj_in0"), sem("adj_in1")]
        stacks_in, stored = sem("stacks_in"), sem("stored")
        dve_step = sem("dve_step")
        act_step = sem("act_step")
        pool_step = sem("pool_step")
        filled = sem("filled")
        sq_ask, sq_done = sem("sq_ask"), sem("sq_done")
        rt_ask, rt_done = sem("rt_ask"), sem("rt_done")
        norm_ready, turned, turned_read, h_kept = map(sem, ("norm_ready", "turned", "turned_read", "h_kept"))
        qk_done, qk_squared, sums_done, roots_done, roots_read, qn_done, qkh_done, qkl_done = map(sem, (
            "qk_done", "qk_squared", "sums_done", "roots_done", "roots_read", "qn_done", "qkh_done", "qkl_done"))
        g_scored, g_exp, g_masked, g_prop, x1_done = map(sem, (
            "g_scored", "g_exp", "g_masked", "g_prop", "x1_done"))
        proj_done, vh_done, v_done, rope_parts, rope_sum, qh_done, ql_done = map(sem, (
            "proj_done", "vh_done", "v_done", "rope_parts", "rope_sum", "qh_done", "ql_done"))
        a_ready, a_free, m_ready, negm_done = map(sem, ("a_ready", "a_free", "m_ready", "negm_done"))
        s_ready, e_ready, eh_ready, el_ready, pv_done, ot_ready = map(sem, (
            "s_ready", "e_ready", "eh_ready", "el_ready", "pv_done", "ot_ready"))
        attn_done = sem("attn_done")
        wh_done, wl_done = sem("wh_done"), sem("wl_done")
        fh_done, fl_done, lg_done, lg_kept = map(sem, ("fh_done", "fl_done", "lg_done", "lg_kept"))
        gate_ready = sem("gate_ready")
        hid_done, silu_done, gated, y_done, acc_done = map(sem, (
            "hid_done", "silu_done", "gated", "y_done", "acc_done"))

        STACKS = 3 * NH + 3 * NKV
        block = ctx.enter_context(nc.Block())
        P2N, P4N = NB, 2 * NB
        RING = 2

        def rows(v, n):
            return v.unsqueeze(2).to_broadcast([P, v.shape[1], n])

        def hidden(u):
            return ps[:, 3 * u:3 * u + 3, :].rearrange("p a c -> p (a c)")

        @block.sync
        def _(sp):
            sp.dma_start(X1[:, :, :], x).then_inc(x_in, 16)
            sp.dma_start(tab[:, :], tables).then_inc(tab_in, 16)
            sp.dma_start(small[:, :], w_small).then_inc(small_in, 16)
            sp.dma_start(tab16[:, :], tables16).then_inc(tab_in, 16)
            hj = NT // 2

            def load_adj(i, slot):
                for k in range(2):
                    sp.dma_start(adj2[:, slot, k * hj:(k + 1) * hj, :],
                                 adj[i, :, k * hj:(k + 1) * hj, :]).then_inc(adj_in[k], 16)
            load_adj(0, 0)
            for k in range(2):
                sp.wait_ge(adj_in[k], 16)
            load_adj(1, 1)
            for i in range(2, NB):
                sp.wait_ge(g_masked, NT * (i - 1) + RING)
                for k in range(2):
                    sp.wait_ge(adj_in[k], 16 * i)
                load_adj(i, i % 2)
            sp.wait_ge(g_masked, NT * NB + RING)
            sp.dma_start(rope_f, rope).then_inc(rope_in, 16)
            sp.wait_ge(ql_done, NB)
            sp.wait_ge(qh_done, NB)
            n = 0
            for h in range(NH):
                for row, part in ((1, QKh), (2, QKh), (3, QKl)):
                    sp.dma_start(Qs[32 * row:32 * row + 32, :, h, :],
                                 part[HD * h:HD * h + HD, 0, :].rearrange("p (b t) -> p b t", b=NB)
                                 ).then_inc(stacks_in, 16)
                    n += 1
            for g in range(NKV):
                for row, part in ((1, QKh), (2, QKl), (3, QKh)):
                    sp.dma_start(Ks[32 * row:32 * row + 32, g, :],
                                 part[HD * g:HD * g + HD, 1, :]).then_inc(stacks_in, 16)
                    n += 1
            assert n == STACKS
            sp.wait_ge(stacks_in, 16 * STACKS)
            sp.dma_start(W1f, w1).then_inc(w_in, 16)
            sp.dma_start(W3f, w3).then_inc(w_in, 16)
            sp.dma_start(W2, w2).then_inc(w2_in, 16)
            sp.wait_ge(acc_done, NE * NB)
            sp.dma_start(out, U[:, :, :]).then_inc(stored, 16)
            sp.wait_ge(stored, 16)

        @block.gpsimd
        def _(pool):
            pool.memset(H1[:, :, C:C + 1], 1.0).then_inc(filled, 1)
            pool.memset(zero16[:, :], 0.0).then_inc(filled, 1)
            pool.memset(bias[:, 0:1], LN_EPS).then_inc(filled, 1)
            pool.memset(bias[:, 1:2], RMS_EPS).then_inc(filled, 1)
            pool.memset(V16[:, :, :, HD:HD + 1], 1.0).then_inc(filled, 1)
            pool.memset(Qs[0:32, :, :, :], 0.0).then_inc(filled, 1)

            def qk_low(i):
                pool.wait_ge(qkh_done, i + 1)
                pool.tensor_tensor(QKl[:, :, bass.ts(i, BT)], qn.rearrange("p (a t) -> p a t", a=2),
                                   QKh[:, :, bass.ts(i, BT)], ALU.subtract).then_inc(qkl_done, 1)
            skewed(pool, NB, [(0, qk_low)])

            def rope_add(i):
                pool.wait_ge(rope_parts, i + 1)
                wait(pool, qh_done, i)
                pool.tensor_tensor(qr, ra, rb, ALU.add).then_inc(rope_sum, 1)

            def q_low(i):
                pool.wait_ge(qh_done, i + 1)
                pool.tensor_tensor(QKl[:, :, bass.ts(i, BT)], qr.rearrange("p (a t) -> p a t", a=2),
                                   QKh[:, :, bass.ts(i, BT)], ALU.subtract).then_inc(ql_done, 1)
                pool.wait_ge(ql_done, i + 1)
            skewed(pool, NB, [(1, q_low), (0, rope_add)])

            pool.wait_ge(rt_ask, 3)
            pool.memset(Ks[0:32, :, :], 0.0).then_inc(pool_step, 1)
            pool.wait_ge(pool_step, 1)
            pool.memset(Ks[0:NH, :, :], 1.0).then_inc(filled, 1)

            n = Count(pool, "tiles", 1)

            def e_low(u):
                pool.wait_ge(eh_ready, n.now())
                pool.wait_ge(pv_done, n.now())
                pool.tensor_tensor(El[u], E[u], Eh[u], ALU.subtract).then_inc(el_ready, 1)
                n.up()

            pool.sem_inc(el_ready, RING)
            e_low(0)
            e_low(1)
            with pool.Fori(1, NB - 1) as i:
                with pool.Fori(0, i + 1):
                    e_low(0)
                    e_low(1)
            for k, (full, high, low) in enumerate(((W1f, W1h, W1l), (W3f, W3h, W3l))):
                pool.wait_ge(wh_done, k + 1)
                pool.tensor_tensor(low, full, high, ALU.subtract).then_inc(wl_done, 1)
            with pool.Fori(0, NB):
                e_low(0)
                e_low(1)

            def f_low(i):
                pool.wait_ge(fh_done, i + 1)
                pool.tensor_tensor(F16l[:, bass.ts(i, BT)], tb[:, :], F16h[:, bass.ts(i, BT)],
                                   ALU.subtract).then_inc(fl_done, 1)
            skewed(pool, NB, [(0, f_low)])

        @block.scalar
        def _(act):
            def squares(n):
                act.wait_ge(sq_ask, n)
                act.activation(SQ, U[:, :, :], ACT.Square).then_inc(sq_done, 1)

            def roots(n, eps):
                act.wait_ge(rt_ask, n)
                act.activation(stat[:, 2, :], stat[:, 1, :], ACT.Sqrt, bias=bias[:, eps:eps + 1],
                               scale=1.0 / C).then_inc(rt_done, 1)

            act.wait_ge(filled, 6)
            squares(1)
            roots(1, 0)

            def turned_copy(i):
                act.wait_ge(turned, i + 1)
                wait(act, qk_done, i)
                act.activation(tb[:, :], ps[:, 0, 0:BT], ACT.Copy).then_inc(turned_read, 1)
                act.activation(H1[:, bass.ts(i, 2), 0:C], nb_[:, :, :], ACT.Copy).then_inc(h_kept, 1)

            def qk_square(i):
                act.wait_ge(qk_done, i + 1)
                wait(act, sums_done, i)
                act.activation(sq, ps[:, 1 + i % 2, :] if isinstance(i, int)
                               else ps[:, bass.ds(1 + i % 2, 1), :].rearrange("p a c -> p (a c)"),
                               ACT.Square).then_inc(qk_squared, 1)

            def qk_root(i):
                act.wait_ge(sums_done, i + 1)
                wait(act, qn_done, i)
                act.activation(nrm, ps[:, 3, :], ACT.Sqrt).then_inc(roots_done, 1)
            skewed(act, NB, [(2, qk_root), (1, qk_square), (0, turned_copy)])

            def g_tile(m, u):
                act.wait_ge(g_scored, m + 1)
                act.wait_ge(g_masked, m + 1)
                act.activation(Eg[u], ps[:, u, 0:BT], ACT.Exp, scale=1.0 / (UNIT * UNIT)).then_inc(g_exp, 1)
            act.sem_inc(g_exp, RING)
            with act.Fori(0, NB) as i:
                with act.Fori(0, NT // 2) as j:
                    for u in range(2):
                        g_tile(i * NT + j * 2 + u, u)

            squares(2)
            roots(2, 0)
            squares(3)
            roots(3, 1)

            def q_turned(i):
                act.wait_ge(turned, P2N + i + 1)
                wait(act, proj_done, i)
                act.activation(tb[:, :], ps[:, 0, 0:BT], ACT.Copy, scale=ln1).then_inc(turned_read, 1)

            def v_high(i):
                act.wait_ge(proj_done, i + 1)
                act.activation(V16[:, bass.ts(i, 2), :, 0:HD],
                               ps[:, 5, 0:2 * NKV * HD].rearrange("p (t g d) -> p t g d", t=2, g=NKV),
                               ACT.Copy).then_inc(vh_done, 1)

            def q_high(i):
                act.wait_ge(rope_sum, i + 1)
                act.activation(QKh[:, :, bass.ts(i, BT)], qr.rearrange("p (a t) -> p a t", a=2),
                               ACT.Copy).then_inc(qh_done, 1)
            skewed(act, NB, [(1, v_high), (1, q_high), (0, q_turned)])

            n = Count(act, "act_tiles", 1)
            done = Count(act, "act_used", RING)

            def exp_tile(u):
                act.wait_ge(s_ready, n.now())
                act.wait_ge(el_ready, n.now())
                act.activation(E[u], ps[:, 2 + 2 * u:4 + 2 * u, :].rearrange("p a c -> p (a c)"),
                               ACT.Exp, scale=SCALE).then_inc(e_ready, 1)
                n.up()
                done.up()

            def out_copy(i):
                act.wait_ge(pv_done, done.now())
                act.activation(OT[0:VW, :, :], ps[0:VW, 6:8, :], ACT.Copy).then_inc(ot_ready, 1)

            act.sem_inc(e_ready, RING)
            exp_tile(0)
            exp_tile(1)
            out_copy(0)
            with act.Fori(1, NB - 1) as i:
                with act.Fori(0, i + 1):
                    exp_tile(0)
                    exp_tile(1)
                out_copy(i)
            act.wait_ge(w_in, 32)
            act.activation(W1h, W1f, ACT.Copy).then_inc(wh_done, 1)
            act.activation(W3h, W3f, ACT.Copy).then_inc(wh_done, 1)
            with act.Fori(0, NB):
                exp_tile(0)
                exp_tile(1)
            out_copy(NB - 1)

            squares(4)
            roots(4, 1)

            def f_turned(i):
                act.wait_ge(turned, P4N + i + 1)
                wait(act, lg_done, i)
                wait(act, fl_done, i)
                act.activation(tb[:, :], ps[:, 0, 0:BT], ACT.Copy, scale=ln2).then_inc(turned_read, 1)

            def keep_logits(i):
                act.wait_ge(lg_done, i + 1)
                act.activation(LG[:, bass.ts(i, 2), :], ps[:, 1, 0:2 * NE].rearrange("p (t e) -> p t e", t=2),
                               ACT.Copy).then_inc(lg_kept, 1)
            skewed(act, NB, [(1, keep_logits), (0, f_turned)])

            act.wait_ge(gate_ready, 1)
            act.activation(R[1][:, :, :], R[0][:, :, :], ACT.Exp).then_inc(act_step, 1)

            def silu(m, u):
                act.wait_ge(hid_done, m + 1)
                act.wait_ge(gated, m + 1)
                act.activation(sl[u], hidden(u)[:, 0:HC * BT], ACT.Silu).then_inc(silu_done, 1)
            with act.Fori(0, NE // 2) as e2:
                with act.Fori(0, NB) as i:
                    for u in range(2):
                        silu(e2 * (2 * NB) + i * 2 + u, u)

        @block.vector
        def _(dve):
            own = Count(dve, "own", 0)

            def link(ins):
                ins.then_inc(dve_step, 1)
                own.up()
                dve.wait_ge(dve_step, own.now())

            def centre(src):
                link(dve.tensor_reduce(stat[:, 0, :], src, X, ALU.add))
                link(dve.tensor_scalar(stat[:, 0, :], stat[:, 0, :], 1.0 / C, None, ALU.mult))
                link(dve.tensor_tensor(U[:, :, :], src, rows(stat[:, 0, :], C), ALU.subtract))

            def row_scale(n):
                dve.sem_inc(sq_ask, 1)
                dve.wait_ge(sq_done, n)
                dve.tensor_reduce(stat[:, 1, :], SQ, X, ALU.add).then_inc(rt_ask, 1)
                dve.wait_ge(rt_done, n)
                link(dve.reciprocal(stat[:, 3, :], stat[:, 2, :]))

            def normalized(i, n, kept):
                wait(dve, turned, n)
                if kept:
                    wait(dve, h_kept, n)
                dve.tensor_tensor(nb_[:, :, :], U[:, bass.ts(i, 2), :],
                                  rows(stat[:, 3, bass.ts(i, 2)], C), ALU.mult).then_inc(norm_ready, 1)

            dve.wait_ge(x_in, 16)
            centre(X1[:, :, :])
            row_scale(1)

            def qk_norm(i):
                dve.wait_ge(roots_done, i + 1)
                wait(dve, qkl_done, i)
                b = ps[:, bass.ds(1 + i % 2, 1), :].rearrange("p a c -> p (a c)")
                link(dve.tensor_scalar(nrm, nrm, COS_EPS, None, ALU.max))
                link(dve.reciprocal(nrm, nrm))
                dve.scalar_tensor_tensor(out=qn, in0=b, scalar=UNIT, in1=nrm, op0=ALU.mult,
                                         op1=ALU.mult).then_inc(qn_done, 1)
                dve.wait_ge(qn_done, i + 1)
                dve.tensor_copy(QKh[:, :, bass.ts(i, BT)],
                                qn.rearrange("p (a t) -> p a t", a=2)).then_inc(qkh_done, 1)
            skewed(dve, NB, [(0, lambda i: normalized(i, i, True)), (2, qk_norm)])

            def mask(i, j, u):
                m = i * NT + j * 2 + u
                dve.wait_ge(g_exp, m + 1 + RING)
                wait(dve, g_prop, m - 1)
                dve.scalar_tensor_tensor(
                    out=Em[u], in0=adj2[:, bass.ds(i % 2, 1), bass.ds(j * 2 + u, 1), :]
                    .rearrange("p a b c -> p (a b c)"), scalar=0.0, in1=Eg[u],
                    op0=ALU.is_gt, op1=ALU.mult).then_inc(g_masked, 1)

            def x_after_graph(i):
                dve.wait_ge(g_prop, NT * (i + 1))
                b = ps[:, bass.ds(4 + i % 2, 1), :].rearrange("p a c -> p (a c)")[:, 0:2 * (C + 1)] \
                    .rearrange("p (t c) -> p t c", t=2)
                has, inv, keep = gs[:, 0:2], gs[:, 2:4], gs[:, 4:6]
                total = b[:, :, C:C + 1].rearrange("p t c -> p (t c)")
                link(dve.tensor_scalar(has, total, 0.0, None, ALU.is_gt))
                link(dve.scalar_tensor_tensor(out=inv, in0=total, scalar=1.0, in1=has, op0=ALU.add,
                                              op1=ALU.subtract))
                link(dve.reciprocal(inv, inv))
                link(dve.scalar_tensor_tensor(out=inv, in0=inv, scalar=0.5, in1=has, op0=ALU.mult, op1=ALU.mult))
                link(dve.tensor_scalar(keep, has, -0.5, 1.0, ALU.mult, ALU.add))
                for t in range(2):
                    link(dve.scalar_tensor_tensor(out=gt[:, t, :], in0=b[:, t, 0:C], scalar=inv[:, t:t + 1],
                                                  in1=X1[:, bass.ds(i * 2 + t, 1), :].rearrange("p a c -> p (a c)"),
                                                  op0=ALU.mult, op1=ALU.add))
                    dve.scalar_tensor_tensor(
                        out=X1[:, bass.ds(i * 2 + t, 1), :].rearrange("p a c -> p (a c)"),
                        in0=H1[:, bass.ds(i * 2 + t, 1), 0:C].rearrange("p a c -> p (a c)"),
                        scalar=keep[:, t:t + 1], in1=gt[:, t, :], op0=ALU.mult, op1=ALU.add).then_inc(x1_done, 1)

            def mask_block(i):
                with dve.Fori(0, NT // 2) as j:
                    for k in range(2):
                        dve.wait_ge(adj_in[k], 16 * (i + 1))
                    for u in range(2):
                        mask(i, j, u)

            dve.sem_inc(g_masked, RING)
            for k in range(2):
                dve.wait_ge(adj_in[k], 16)
            mask(0, 0, 0)
            mask(0, 0, 1)
            with dve.Fori(1, NT // 2) as j:
                for u in range(2):
                    mask(0, j, u)
            with dve.Fori(1, NB) as i:
                mask_block(i)
                x_after_graph(i - 1)
            x_after_graph(NB - 1)

            dve.wait_ge(x1_done, 2 * NB)
            centre(X1[:, :, :])
            row_scale(2)
            link(dve.tensor_tensor(U[:, :, :], U[:, :, :], rows(stat[:, 3, :], C), ALU.mult))
            row_scale(3)

            def rope_halves(i):
                dve.wait_ge(proj_done, i + 1)
                wait(dve, rope_sum, i)
                for k, dst in ((0, ra), (1, rb)):
                    ins = dve.tensor_tensor(dst.rearrange("p (a t) -> p a t", a=2),
                                            ps[:, 1 + k, :].rearrange("p (a t) -> p a t", a=2),
                                            rope_f[:, k, bass.ts(i, BT)].unsqueeze(1).to_broadcast([P, 2, BT]),
                                            ALU.mult)
                ins.then_inc(rope_parts, 1)

            def v_low(i):
                dve.wait_ge(vh_done, i + 1)
                dve.tensor_tensor(V16[:, bass.ts(i, 2), :, HD + 1:VW],
                                  ps[:, 5, 0:2 * NKV * HD].rearrange("p (t g d) -> p t g d", t=2, g=NKV),
                                  V16[:, bass.ts(i, 2), :, 0:HD], ALU.subtract).then_inc(v_done, 1)
            dve.wait_ge(rope_in, 16)
            skewed(dve, NB, [(0, lambda i: normalized(i, P2N + i, False)), (1, rope_halves), (1, v_low)])

            a = Count(dve, "a", 1)
            a_freed = Count(dve, "a_freed", RING)
            n = Count(dve, "tiles", 1)
            n_e = Count(dve, "tiles_e", 1 + RING)

            def a_bank(s):
                return ps[:, s, :]

            def chunk_max(j):
                for t in range(2):
                    for g in range(NKV):
                        dve.wait_ge(a_ready, a.now())
                        dve.tensor_reduce(cm[:, t, 2 * g:2 * g + 2, bass.ds(j, 1)].rearrange("p h j -> p (h j)"),
                                          a_bank(g).rearrange("p (h k) -> p h k", h=2), X, ALU.max
                                          ).then_inc(a_free, 1)
                        a.up()
                        a_freed.up()

            def block_max(i):
                dve.wait_ge(a_free, a_freed.now())
                dve.tensor_reduce(m8[:, :, :].rearrange("p t h -> p (t h)"),
                                  cm[:, :, :, :].rearrange("p t h j -> p (t h) j"), X, ALU.max).then_inc(m_ready, 1)
                for t in range(2):
                    dve.wait_ge(a_ready, a.now())
                    dve.tensor_tensor(Qs[0:NH, bass.ds(i, 1), :, t * P:t * P + P].rearrange("p a h t -> p (a h) t"),
                                      a_bank(t)[0:NH, 0:P].unsqueeze(1).to_broadcast([NH, NH, P]),
                                      negblk, ALU.mult).then_inc(a_free, 1)
                    a.up()
                    a_freed.up()
                dve.wait_ge(a_free, a_freed.now())
                dve.sem_inc(negm_done, 1)

            def e_high(u):
                dve.wait_ge(e_ready, n_e.now())
                dve.wait_ge(pv_done, n.now())
                dve.tensor_copy(Eh[u], E[u]).then_inc(eh_ready, 1)
                n.up()
                n_e.up()

            def attention_out(i):
                for t in range(2):
                    ut = U[:, bass.ds(i * 2 + t, 1), :].rearrange("p a c -> p (a c)")
                    for g in range(NKV):
                        dve.wait_ge(a_ready, a.now())
                        z = a_bank(g)[:, 0:2 * (C + 1)].rearrange("p (h c) -> p h c", h=2)
                        link(dve.reciprocal(zr[:, :], z[:, :, C:C + 1].rearrange("p h c -> p (h c)")))
                        link(dve.scalar_tensor_tensor(out=ut, in0=z[:, 0, 0:C], scalar=zr[:, 0:1], in1=ut,
                                                      op0=ALU.mult, op1=ALU.add))
                        link(dve.scalar_tensor_tensor(out=ut, in0=z[:, 1, 0:C], scalar=zr[:, 1:2], in1=ut,
                                                      op0=ALU.mult, op1=ALU.add))
                        dve.sem_inc(a_free, 1)
                        a.up()
                        a_freed.up()

            def reset_max():
                dve.wait_ge(m_ready, mx.now())
                link(dve.memset(cm[:, :, :, :], LOWEST))

            mx = Count(dve, "mx", 0)
            dve.sem_inc(a_free, RING)
            dve.sem_inc(pv_done, RING)
            dve.sem_inc(gated, RING)
            link(dve.memset(cm[:, :, :, :], LOWEST))
            chunk_max(0)
            block_max(0)
            mx.up()

            def attention_block(i, after, before):
                if after:
                    reset_max()
                    chunk_max(i + 1)
                e_high(0)
                e_high(1)
                if before:
                    attention_out(i - 1)
                    with dve.Fori(0, i) as j:
                        if after:
                            chunk_max(j)
                        e_high(0)
                        e_high(1)
                if after:
                    chunk_max(i)
                    block_max(i + 1)
                    mx.up()

            attention_block(0, True, False)
            with dve.Fori(1, NB - 1) as i:
                attention_block(i, True, True)
            attention_block(NB - 1, False, True)
            attention_out(NB - 1)

            row_scale(4)

            def f_high(i):
                dve.wait_ge(turned_read, P4N + i + 1)
                dve.tensor_copy(F16h[:, bass.ts(i, BT)], tb[:, :]).then_inc(fh_done, 1)
            skewed(dve, NB, [(0, lambda i: normalized(i, P4N + i, False)), (1, f_high)])

            dve.wait_ge(lg_kept, NB)
            big, tot, r = rs[:, 0, :], rs[:, 1, :], R
            revb = rev.unsqueeze(1).to_broadcast([P, NT, NE])
            link(dve.tensor_reduce(big, LG[:, :, :], X, ALU.max))
            dve.tensor_tensor(r[0][:, :, :], LG[:, :, :], rows(big, NE), ALU.subtract).then_inc(gate_ready, 1)
            dve.wait_ge(act_step, 1)
            link(dve.tensor_reduce(tot, r[1][:, :, :], X, ALU.add))
            link(dve.reciprocal(tot, tot))
            link(dve.tensor_tensor(r[1][:, :, :], r[1][:, :, :], rows(tot, NE), ALU.mult))

            def first_largest(probs, dst, top, pick):
                link(dve.tensor_reduce(top, probs, X, ALU.max))
                link(dve.tensor_tensor(dst, probs, rows(top, NE), ALU.is_equal))
                link(dve.tensor_tensor(dst, dst, revb, ALU.mult))
                link(dve.tensor_reduce(pick, dst, X, ALU.max))
                link(dve.tensor_tensor(dst, dst, rows(pick, NE), ALU.is_equal))
            first_largest(r[1][:, :, :], r[0][:, :, :], rs[:, 2, :], rs[:, 3, :])
            link(dve.scalar_tensor_tensor(out=r[2][:, :, :].rearrange("p t e -> p (t e)"),
                                          in0=r[0][:, :, :].rearrange("p t e -> p (t e)"), scalar=-2.0,
                                          in1=r[1][:, :, :].rearrange("p t e -> p (t e)"),
                                          op0=ALU.mult, op1=ALU.add))
            first_largest(r[2][:, :, :], r[3][:, :, :], rs[:, 4, :], rs[:, 5, :])
            link(dve.tensor_tensor(r[0][:, :, :], r[0][:, :, :], r[3][:, :, :], ALU.add))
            link(dve.scalar_tensor_tensor(out=tot, in0=rs[:, 2, :], scalar=1e-9, in1=rs[:, 4, :],
                                          op0=ALU.add, op1=ALU.add))
            link(dve.reciprocal(tot, tot))
            link(dve.tensor_tensor(r[0][:, :, :], r[0][:, :, :], r[1][:, :, :], ALU.mult))
            link(dve.tensor_tensor(GW[:, :, :], r[0][:, :, :], rows(tot, NE), ALU.mult))
            link(dve.tensor_tensor(U[:, :, :], U[:, :, :], X1[:, :, :], ALU.add))

            def gate(m, u):
                dve.wait_ge(silu_done, m + 1)
                wait(dve, y_done, m - 1)
                dve.tensor_tensor(hh_[u], hidden(u)[:, HC * BT:2 * HC * BT], sl[u], ALU.mult).then_inc(gated, 1)

            def add_expert(m, e, i, u):
                dve.wait_ge(y_done, m + 1)
                wait(dve, acc_done, m)
                for t in range(2):
                    ut = U[:, bass.ds(i * 2 + t, 1), :].rearrange("p a c -> p (a c)")
                    ins = dve.scalar_tensor_tensor(
                        out=ut, in0=ps[:, 6 + u, t * C:(t + 1) * C],
                        scalar=GW[:, bass.ds(i * 2 + t, 1), bass.ds(e, 1)].rearrange("p a c -> p (a c)"),
                        in1=ut, op0=ALU.mult, op1=ALU.add)
                ins.then_inc(acc_done, 1)

            def expert_turn(e2, i, nxt):
                m = e2 * (2 * NB) + i * 2
                gate(m + 1, 1)
                add_expert(m, e2 * 2, i, 0)
                if nxt:
                    gate(m + 2, 0)
                add_expert(m + 1, e2 * 2 + 1, i, 1)

            gate(0, 0)
            expert_turn(0, 0, True)
            with dve.Fori(1, NB) as i:
                expert_turn(0, i, True)
            with dve.Fori(1, NE // 2 - 1) as e2:
                with dve.Fori(0, NB) as i:
                    expert_turn(e2, i, True)
            with dve.Fori(0, NB - 1) as i:
                expert_turn(NE // 2 - 1, i, True)
            expert_turn(NE // 2 - 1, NB - 1, False)

        @block.tensor
        def _(pe):
            def turn(n):
                pe.wait_ge(norm_ready, n + 1)
                wait(pe, turned_read, n)
                for t in range(2):
                    ins = pe.transpose(ps[:, 0, t * P:(t + 1) * P], nb_[:, t, :], ident)
                ins.then_inc(turned, 1)

            pe.wait_ge(tab_in, 32)
            pe.wait_ge(small_in, 16)
            pe.wait_ge(filled, 6)

            def qk(i):
                pe.wait_ge(turned_read, i + 1)
                wait(pe, qn_done, i - 1)
                for k in range(2):
                    ins = pe.matmul(ps[:, bass.ds(1 + i % 2, 1), k * BT:(k + 1) * BT].rearrange("p a c -> p (a c)"),
                                    Wqk[:, k * C:(k + 1) * C], tb[:, :], start=True, stop=True)
                ins.then_inc(qk_done, 1)

            def row_sums(i):
                pe.wait_ge(qk_squared, i + 1)
                wait(pe, roots_done, i)
                pe.matmul(ps[:, 3, :], ones, sq, start=True, stop=True).then_inc(sums_done, 1)
            skewed(pe, NB, [(2, row_sums), (1, qk), (0, turn)])

            def g_scores(i, jt, u, m):
                pe.wait_ge(g_exp, m + 1)
                q = slice(0, 1)
                parts = ((QKh, QKh), (QKh, QKl), (QKl, QKh))
                for k, (qa, ka) in enumerate(parts):
                    ins = pe.matmul(ps[:, u, 0:BT], qa[:, 0, bass.ts(jt, P)], ka[:, 1, bass.ts(i, BT)],
                                    start=(k == 0), stop=(k == len(parts) - 1))
                ins.then_inc(g_scored, 1)

            def g_bank(i):
                return ps[:, bass.ds(4 + i % 2, 1), :].rearrange("p a c -> p (a c)")

            def g_clear(i):
                wait(pe, x1_done, (i - 1) * 2)
                pe.matmul(g_bank(i)[:, 0:2 * (C + 1)], zero16[:, 0:P], zero16[:, 0:2 * (C + 1)],
                          start=True, stop=False, skip_group_check=True)

            def g_propagate(i, jt, u, m):
                pe.wait_ge(g_masked, m + 1 + RING)
                for t in range(2):
                    ins = pe.matmul(g_bank(i)[:, t * (C + 1):(t + 1) * (C + 1)], Em[u][:, t * P:(t + 1) * P],
                                    H1[:, bass.ds(jt, 1), :].rearrange("p a c -> p (a c)"),
                                    start=False, stop=False, skip_group_check=True)
                ins.then_inc(g_prop, 1)

            def g_block(i, nxt):
                g_clear(i)
                with pe.Fori(0, NT // 2 - 1) as j:
                    for u in range(2):
                        m = i * NT + j * 2 + u
                        g_propagate(i, j * 2 + u, u, m)
                        g_scores(i, j * 2 + 2 + u, u, m + 2)
                for u in range(2):
                    m = i * NT + (NT - 2) + u
                    g_propagate(i, NT - 2 + u, u, m)
                    if nxt:
                        g_scores(i + 1, u, u, m + 2)

            pe.wait_ge(qkl_done, NB)
            pe.wait_ge(qkh_done, NB)
            pe.wait_ge(h_kept, NB)
            for u in range(2):
                g_scores(0, u, u, u)
            g_block(0, True)
            g_block(1, True)
            with pe.Fori(2, NB - 1) as i:
                g_block(i, True)
            g_block(NB - 1, False)

            def project(i):
                pe.wait_ge(turned_read, P2N + i + 1)
                wait(pe, rope_parts, i)
                wait(pe, v_done, i)
                for k in range(4):
                    pe.matmul(ps[:, 1 + k // 2, (k % 2) * BT:(k % 2 + 1) * BT], Wf[:, k * P:(k + 1) * P], tb[:, :],
                              start=True, stop=True)
                for t in range(2):
                    ins = pe.matmul(ps[:, 5, t * NKV * HD:(t + 1) * NKV * HD], tb[:, t * P:(t + 1) * P], Wv,
                                    start=True, stop=True)
                ins.then_inc(proj_done, 1)
            skewed(pe, NB, [(1, project), (0, lambda i: turn(P2N + i))])

            pe.wait_ge(stacks_in, 16 * STACKS)
            pe.wait_ge(filled, 7)
            a = Count(pe, "a_slot", 1)
            s = Count(pe, "s_slot", 1)
            v = Count(pe, "v_tile", 1 + RING)

            def a_task(u, fill):
                pe.wait_ge(a_free, a.now())
                fill(ps[:, u, :]).then_inc(a_ready, 1)
                a.up()

            def row_chunk(i, j, diagonal):
                for t in range(2):
                    for g in range(NKV):
                        def fill(bank):
                            if diagonal:
                                pe.matmul(bank, ident16, maskA[:, t, :], start=True, stop=False,
                                          skip_group_check=True)
                            for h in range(2):
                                ins = pe.matmul(bank[:, h * BT:(h + 1) * BT],
                                                Qs[:, bass.ds(i, 1), 2 * g + h, t * P:(t + 1) * P]
                                                .rearrange("p a t -> p (a t)"),
                                                Ks[:, g, bass.ts(j, BT)], start=not diagonal, stop=True,
                                                skip_group_check=True)
                            return ins
                        a_task(g, fill)

            def maxima(i):
                pe.wait_ge(m_ready, i + 1)
                for t in range(2):
                    a_task(t, lambda bank: pe.transpose(bank[0:NH, 0:P], m8[:, t, :], ident))

            def scores(i, jt, u, diagonal):
                pe.wait_ge(e_ready, s.now())
                for g in range(NKV):
                    bank = ps[:, 2 + 2 * u + g, :]
                    ins = pe.matmul(bank, Ks[:, g, bass.ts(jt, P)],
                                    Qs[:, bass.ds(i, 1), 2 * g:2 * g + 2, :].rearrange("p a h t -> p (a h t)"),
                                    start=True, stop=not diagonal)
                    if diagonal:
                        ins = pe.matmul(bank, ident16, maskB[:, u, :], start=False, stop=True)
                ins.then_inc(s_ready, 1)
                s.up()

            def values(jt, u):
                pe.wait_ge(el_ready, v.now())
                for part in (Eh[u], El[u]):
                    for g in range(NKV):
                        ins = pe.matmul(ps[0:VW, 6 + g, :], V16[:, bass.ds(jt, 1), g, :].rearrange("p a c -> p (a c)"),
                                        part[:, g * 512:(g + 1) * 512], start=False, stop=False,
                                        skip_group_check=True)
                ins.then_inc(pv_done, 1)
                v.up()

            def through_wo(i):
                for t in range(2):
                    for g in range(NKV):
                        def fill(bank):
                            for h in range(2):
                                ins = pe.matmul(bank[:, h * (C + 1):(h + 1) * (C + 1)],
                                                OT[0:VW, g, h * BT + t * P:h * BT + (t + 1) * P],
                                                WoA[:, 2 * g + h, :], start=True, stop=True)
                            return ins
                        a_task(g, fill)

            def attention_block(i, after, before):
                wait(pe, negm_done, i + 1)
                for u in range(2):
                    scores(i, i * 2 + u, u, True)
                if after:
                    row_chunk(i + 1, i + 1, True)
                if before:
                    pe.wait_ge(ot_ready, i)
                    through_wo(i - 1)
                for g in range(NKV):
                    pe.matmul(ps[0:VW, 6 + g, :], zero16[:, 0:VW], zero16[:, :], start=True, stop=False,
                              skip_group_check=True)
                if before:
                    pe.reg_mov(last, i)
                    with pe.Fori(0, i) as j:
                        for u in range(2):
                            scores(i, j * 2 + u, u, False)
                        if after:
                            row_chunk(i + 1, j, False)
                        for u in range(2):
                            values(pe.snap(last) * 2 + u, u)
                        pe.reg_mov(last, j)
                if after:
                    row_chunk(i + 1, i, False)
                for u in range(2):
                    values((i - 1) * 2 + u if before else u, u)
                if after:
                    maxima(i + 1)

            last = pe.alloc_register("last_pair")
            row_chunk(0, 0, True)
            maxima(0)
            attention_block(0, True, False)
            with pe.Fori(1, NB - 1) as i:
                attention_block(i, True, True)
            attention_block(NB - 1, False, True)
            pe.wait_ge(ot_ready, NB)
            through_wo(NB - 1)

            def route(i):
                pe.wait_ge(turned_read, P4N + i + 1)
                wait(pe, lg_kept, i)
                for t in range(2):
                    ins = pe.matmul(ps[:, 1, t * NE:(t + 1) * NE], tb[:, t * P:(t + 1) * P], Wr,
                                    start=True, stop=True)
                ins.then_inc(lg_done, 1)
            skewed(pe, NB, [(1, route), (0, lambda i: turn(P4N + i))])

            pe.wait_ge(fl_done, NB)
            pe.wait_ge(fh_done, NB)
            pe.wait_ge(wl_done, 2)
            pe.wait_ge(w2_in, 16)
            pe.wait_ge(lg_kept, NB)

            def hidden_rows(m, e, i, u):
                pe.wait_ge(gated, m + 1)
                for k, (wh, wl) in enumerate(((W1h, W1l), (W3h, W3l))):
                    for c in range(HC):
                        dst = hidden(u)[:, (k * HC + c) * BT:(k * HC + c + 1) * BT]
                        parts = ((wh, F16h), (wh, F16l), (wl, F16h))
                        for q, (wa, fa) in enumerate(parts):
                            ins = pe.matmul(dst, wa[:, bass.ds(e * HW + c * P, P)], fa[:, bass.ts(i, BT)],
                                            start=(q == 0), stop=(q == len(parts) - 1))
                ins.then_inc(hid_done, 1)

            def expert_out(m, e, u):
                pe.wait_ge(gated, m + 1 + RING)
                wait(pe, acc_done, m - 1)
                for t in range(2):
                    for c in range(HC):
                        ins = pe.matmul(ps[:, 6 + u, t * C:(t + 1) * C],
                                        hh_[u][:, c * BT + t * P:c * BT + (t + 1) * P],
                                        W2[:, bass.ds((e * HC + c) * C, C)],
                                        start=(c == 0), stop=(c == HC - 1))
                ins.then_inc(y_done, 1)

            def expert_turn(e2, i, nxt):
                m = e2 * (2 * NB) + i * 2
                hidden_rows(m + 1, e2 * 2 + 1, i, 1)
                expert_out(m, e2 * 2, 0)
                if nxt:
                    hidden_rows(m + 2, nxt[0] * 2, nxt[1], 0)
                expert_out(m + 1, e2 * 2 + 1, 1)

            hidden_rows(0, 0, 0, 0)
            expert_turn(0, 0, (0, 1))
            with pe.Fori(1, NB - 1) as i:
                expert_turn(0, i, (0, i + 1))
            expert_turn(0, NB - 1, (1, 0))
            with pe.Fori(1, NE // 2 - 1) as e2:
                with pe.Fori(0, NB - 1) as i:
                    expert_turn(e2, i, (e2, i + 1))
                expert_turn(e2, NB - 1, (e2 + 1, 0))
            with pe.Fori(0, NB - 1) as i:
                expert_turn(NE // 2 - 1, i, (NE // 2 - 1, i + 1))
            expert_turn(NE // 2 - 1, NB - 1, None)


def shape_tables():
    p = np.arange(P)[:, None]
    ident = np.eye(P, dtype=np.float32)
    negblk = np.zeros((P, NH, P), np.float32)
    for h in range(NH):
        negblk[h, h, :] = -1.0
    rev = np.tile(np.arange(NE, 0, -1, dtype=np.float32), (P, 1))
    tables = np.concatenate([ident, np.ones((P, P), np.float32), negblk.reshape(P, -1), rev], axis=1)
    k = np.arange(BT)[None, :]
    mask_a = np.stack([np.tile(np.where(k <= t * P + p, 0.0, FAR), (1, 2)) for t in range(2)], axis=1)
    mask_b = np.stack([np.tile(np.where(k >= t * P + p, 0.0, FAR), (1, 2)) for t in range(2)], axis=1)
    tables16 = np.concatenate([ident, mask_a.reshape(P, -1), mask_b.reshape(P, -1)], axis=1).astype(np.float16)
    inv_freq = 1.0 / 10000.0 ** (np.arange(0, HD, 2, dtype=np.float32) / HD)
    freqs = np.outer(np.arange(TP, dtype=np.float32), inv_freq)
    emb = np.concatenate([freqs, freqs], axis=-1)
    cos, sin = np.cos(emb).T, np.sin(emb).T
    sin = np.concatenate([-sin[:HD // 2], sin[HD // 2:]], axis=0)
    rope = np.stack([np.tile(cos, (P // HD, 1)), np.tile(sin, (P // HD, 1))], axis=1).astype(np.float32)
    return tables, tables16, rope


def kernel(x, adj, L0_gnn_Wq, L0_gnn_Wk, L0_ffn_ln1_w, L0_ffn_ln2_w, L0_ffn_wq, L0_ffn_wk, L0_ffn_wv,
           L0_ffn_wo, L0_ffn_router_w, L0_ffn_w1, L0_ffn_w2, L0_ffn_w3):
    import concourse.bacc as bacc
    from concourse.bass_utils import run_bass_kernel_spmd

    f = lambda v: np.asarray(v)
    tables, tables16, rope = shape_tables()
    pad = TP - NTOK
    xs = np.pad(f(x), ((0, pad), (0, 0))).reshape(NT, P, C).transpose(1, 0, 2)
    adj_t = np.pad(f(adj), ((0, pad), (0, pad))).reshape(NB, BT, NT, P).transpose(0, 3, 2, 1)

    wq, wk, wo = f(L0_ffn_wq), f(L0_ffn_wk), f(L0_ffn_wo)
    partner = lambda w: w.reshape(-1, 2, HD // 2, C)[:, ::-1].reshape(w.shape)
    to_p = lambda w: np.pad(w, ((0, P - w.shape[0]), (0, 0))).T
    wo_aug = np.zeros((P, NH, C + 1), np.float32)
    for h in range(NH):
        head = wo[:, h * HD:(h + 1) * HD].T
        wo_aug[0:HD, h, 0:C] = head
        wo_aug[HD, h, C] = 1.0
        wo_aug[HD + 1:VW, h, 0:C] = head
    w_small = np.concatenate([
        f(L0_gnn_Wq).T, f(L0_gnn_Wk).T, to_p(wq), to_p(wk), to_p(partner(wq)), to_p(partner(wk)),
        f(L0_ffn_wv).T, f(L0_ffn_router_w).T, wo_aug.reshape(P, -1),
        f(L0_ffn_ln1_w)[:, None], f(L0_ffn_ln2_w)[:, None]], axis=1)
    up = lambda w: np.pad(f(w), ((0, 0), (0, HW - HID), (0, 0))).transpose(2, 0, 1).reshape(C, NE * HW)
    down = np.pad(f(L0_ffn_w2), ((0, 0), (0, 0), (0, HW - HID))) \
        .reshape(NE, C, HC, P).transpose(3, 0, 2, 1).reshape(P, NE * HC * C)
    arrays = {"x": xs, "adj": adj_t, "w_small": w_small, "w1": up(L0_ffn_w1), "w3": up(L0_ffn_w3), "w2": down,
              "rope": rope, "tables": tables, "tables16": tables16}
    arrays = {f"in_{k}": np.ascontiguousarray(v) for k, v in arrays.items()}

    nc = bacc.Bacc("TRN2", target_bir_lowering=False, num_devices=1)
    args = [nc.dram_tensor(k, v.shape, mybir.dt.from_np(v.dtype), kind="ExternalInput").ap()
            for k, v in arrays.items()]
    args.append(nc.dram_tensor("out", (P, NT, C), F32, kind="ExternalOutput").ap())
    graph_ffn_program(nc, *args)
    r = run_bass_kernel_spmd(nc, [arrays], core_ids=[0])
    return r.results[0]["out"].transpose(1, 0, 2).reshape(TP, C)[:NTOK]
```

```python
from contextlib import ExitStack

import numpy as np

import concourse.bass as bass
from concourse import mybir

F32 = mybir.dt.float32
F16 = mybir.dt.float16
I32 = mybir.dt.int32
ALU = mybir.AluOpType
ACT = mybir.ActivationFunctionType
X = mybir.AxisListType.X

P = 128
NTOK = 3327
C = 128
NT = -(-NTOK // P)
NB = NT // 2
BT = 2 * P
TP = NT * P
NH, NKV, HD = 4, 2, 32
PC = 640
VW = 2 * HD + 1
NE = 8
HID = int(8 / 3 * C)
HC = -(-HID // P)
HW = HC * P
LN_EPS = 1e-5
RMS_EPS = 1e-6
COS_EPS = 1e-4
UNIT = 64.0
SCALE = float(HD) ** -0.5
FAR = -60000.0
LOWEST = -3.0e38


class Count:

    def __init__(self, eng, name, start):
        self.eng = eng
        self.reg = eng.alloc_register(name)
        eng.reg_mov(self.reg, start)

    def up(self, by=1):
        self.eng.reg_add(self.reg, self.reg, by)

    def now(self):
        return self.reg


def wait(eng, sem, value):
    if isinstance(value, int) and value <= 0:
        return
    eng.wait_ge(sem, value)


def skewed(eng, n, stages):
    most = max(lag for lag, _ in stages)
    lead = most + 2
    for k in range(lead):
        for lag, stage in stages:
            if k >= lag:
                stage(k - lag)
    with eng.Fori(lead, n) as k:
        for lag, stage in stages:
            stage(k - lag)
    for k in range(n, n + most):
        for lag, stage in stages:
            if k - lag < n:
                stage(k - lag)


def graph_ffn_program(nc, x, adj, w_small, w1, w3, w2, rope, tables, tables16, out):
    ctx = ExitStack()
    with ctx:
        def sb(name, shape, dt):
            return ctx.enter_context(nc.sbuf_tensor(name, shape, dt))

        def sem(name):
            return ctx.enter_context(nc.semaphore(name))

        X1 = sb("X1", [P, NT, C], F32)
        H1 = sb("H1", [P, NT, C + 1], F32)
        U = sb("U", [P, NT, C], F32)
        adj_bytes = sb("adj_bytes", [P, 2 * NT * BT], I32)
        half_bytes = sb("half_bytes", [P, 4 * TP], F16)
        Qs = sb("Qs", [P, NB, NH, BT], F16)
        Ks = sb("Ks", [P, NKV, TP], F16)
        V16 = sb("V16", [P, NT, NKV, VW], F16)
        adj2 = adj_bytes[:, :].rearrange("p (s t c) -> p s t c", s=2, t=NT)
        rope_f = adj_bytes[:, 0:2 * TP].bitcast(F32).rearrange("p (a t) -> p a t", a=2)
        moe_bytes = adj_bytes[:, :].bitcast(F16)
        ew = NE * HW
        W1h, W1l, W3h, W3l = (moe_bytes[:, k * ew:(k + 1) * ew] for k in range(4))
        F16h = moe_bytes[:, 4 * ew:4 * ew + TP]
        F16l = moe_bytes[:, 4 * ew + TP:4 * ew + 2 * TP]
        w2_at = 4 * ew + 2 * TP
        W2h, W2l = (moe_bytes[:, w2_at + k * ew:w2_at + (k + 1) * ew] for k in range(2))
        QKh = half_bytes[:, 0:2 * TP].rearrange("p (a t) -> p a t", a=2)
        QKl = half_bytes[:, 2 * TP:4 * TP].rearrange("p (a t) -> p a t", a=2)
        W1f = half_bytes[:, 0:2 * ew].bitcast(F32)
        W3f = half_bytes[:, 2 * ew:4 * ew].bitcast(F32)
        W2f = W1f

        small = sb("small", [P, w_small.shape[1]], F32)
        at = 0
        def cut(n, rows=P):
            nonlocal at
            at += n
            return small[0:rows, at - n:at]
        Wqk = cut(2 * C)
        Wf = cut(4 * P)
        Wv = cut(NKV * HD)
        Wr = cut(NE)
        WoA = cut(NH * (C + 1), VW).rearrange("p (h c) -> p h c", h=NH)
        ln1 = cut(1)
        ln2 = cut(1)
        tab = sb("tab", [P, tables.shape[1]], F32)
        ident = tab[:, 0:P]
        ones = tab[:, P:2 * P]
        negblk = tab[0:NH, 2 * P:2 * P + NH * P].rearrange("p (h t) -> p h t", h=NH)
        rev = tab[:, 2 * P + NH * P:2 * P + NH * P + NE]
        tab16 = sb("tab16", [P, tables16.shape[1]], F16)
        ident16 = tab16[:, 0:P]
        maskA = tab16[:, P:P + 1024].rearrange("p (t c) -> p t c", t=2)
        maskB = tab16[:, P + 1024:P + 2048].rearrange("p (t c) -> p t c", t=2)
        zero16 = sb("zero16", [P, 512], F16)

        stat = sb("stat", [P, 8, NT], F32)
        bias = sb("bias", [P, 2], F32)
        unused = sb("unused", [P, 1], F32)
        nb_ = sb("nb", [P, 2, C], F32)
        tb = sb("tb", [P, BT], F32)
        tmp = sb("tmp", [P, 4096], F32)
        sq, qn = tmp[:, 0:512], tmp[:, 512:1024]
        ra, rb, qr = tmp[:, 0:512], tmp[:, 512:1024], tmp[:, 1024:1536]
        Eg = [tmp[:, 1024 + 256 * k:1280 + 256 * k] for k in range(2)]
        Em = [tmp[:, 1536 + 256 * k:1792 + 256 * k] for k in range(2)]
        EH = [tmp[:, 512 * k:512 * k + 512].bitcast(F16) for k in range(2)]
        EL = [tmp[:, 1024 + 512 * k:1536 + 512 * k].bitcast(F16) for k in range(2)]
        h_bytes = H1[:, :, :].rearrange("p t c -> p (t c)")
        E = [h_bytes[:, 1024 * k:1024 * k + 1024] for k in range(2)]
        sl = [tmp[:, 768 * k:768 * k + 768] for k in range(2)]
        hh_ = [tmp[:, 1536 + 768 * k:2304 + 768 * k] for k in range(2)]
        hhh = [h_bytes[:, 384 * k:384 * k + 384].bitcast(F16) for k in range(2)]
        hhl = [h_bytes[:, 768 + 384 * k:1152 + 384 * k].bitcast(F16) for k in range(2)]
        st6 = sb("st6", [P, NT, 6], F32)
        ss4 = sb("ss4", [P, 2, 4], F32)
        gs = sb("gs", [P, 8], F32)
        gt = sb("gt", [P, 2, C], F32)
        OT = sb("OT", [P, NKV, 512], F32)
        cm = sb("cm", [P, 2, NH, NB], F32)
        m8 = sb("m8", [P, 2, NH], F32)
        zr = sb("zr", [P, 2], F32)
        LG = sb("LG", [P, NT, NE], F32)
        R = [sb(f"R{k}", [P, NT, NE], F32) for k in range(4)]
        GW = sb("GW", [P, NT, NE], F32)
        rs = sb("rs", [P, 6, NT], F32)

        ps = ctx.enter_context(nc.psum_tensor("ps", [P, 8, 512], F32))

        x_in, x_in2, small_in, tab_in, rope_in, w_in, w2_in = map(sem, (
            "x_in", "x_in2", "small_in", "tab_in", "rope_in", "w_in", "w2_in"))
        adj_in = [sem("adj_in0"), sem("adj_in1")]
        stacks_in, stored = [sem("stacks_in0"), sem("stacks_in1")], sem("stored")
        dve_step = sem("dve_step")
        act_step = sem("act_step")
        table_in = sem("table_in")
        pool_step = sem("pool_step")
        filled = sem("filled")
        rt_ask, rt_done = sem("rt_ask"), sem("rt_done")
        norm_ready, turned, turned_read, h_kept = map(sem, ("norm_ready", "turned", "turned_read", "h_kept"))
        qk_done, qk_squared, sums_done, roots_done, qn_done, qn_turned, qkh_done, qkl_done = map(sem, (
            "qk_done", "qk_squared", "sums_done", "roots_done", "qn_done", "qn_turned", "qkh_done", "qkl_done"))
        g_scored, g_exp, g_masked, g_prop, x1_done = map(sem, (
            "g_scored", "g_exp", "g_masked", "g_prop", "x1_done"))
        stats_done, u_done = sem("stats_done"), sem("u_done")
        proj_done, vh_done, v_done, rope_parts, rope_sum, qh_done, ql_done = map(sem, (
            "proj_done", "vh_done", "v_done", "rope_parts", "rope_sum", "qh_done", "ql_done"))
        a_ready, a_free, m_ready, negm_done = map(sem, ("a_ready", "a_free", "m_ready", "negm_done"))
        e_full = sem("e_full")
        s_ready, e_ready, el_pool, el_dve, pv_done, ot_ready = map(sem, (
            "s_ready", "e_ready", "el_pool", "el_dve", "pv_done", "ot_ready"))
        wh_done, wl_done = sem("wh_done"), sem("wl_done")
        fh_done, fl_done, lg_done, lg_kept = map(sem, ("fh_done", "fl_done", "lg_done", "lg_kept"))
        gate_ready = sem("gate_ready")
        hid_done, silu_done, gated, gated_high, gated_low, y_done, acc_done = map(sem, (
            "hid_done", "silu_done", "gated", "gated_high", "gated_low", "y_done", "acc_done"))

        STACKS = 3 * NH + 3 * NKV
        STACKED = [(0, 4), (4, NB)]
        STORED = [(0, 7), (7, 11), (11, NB)]
        block = ctx.enter_context(nc.Block())
        W13_BLOCK = NB - 3
        P2N, P4N = NB, 2 * NB
        RING = 2

        def rows(v, n):
            return v.unsqueeze(2).to_broadcast([P, v.shape[1], n])

        def nat(i):
            return ps[:, bass.ds(1 + i % 2, 1), :].rearrange("p a c -> p (a c)")

        def qk_banks(i, k):
            return ps[:, bass.ds(1 + i % 2 * 2 + k, 1), :].rearrange("p a c -> p (a c)")

        def v_bank(i):
            return ps[:, bass.ds(5 + i % 2, 1), 0:2 * NKV * HD].rearrange("p a (t g d) -> p (a t) g d", t=2, g=NKV)

        def hidden(u):
            return ps[:, 3 * u:3 * u + 3, :].rearrange("p a c -> p (a c)")

        @block.sync
        def _(sp):
            ht = NT // 2
            sp.dma_start(X1[:, 0:ht, :], x[:, 0:ht, :]).then_inc(x_in, 16)
            sp.dma_start(X1[:, ht:NT, :], x[:, ht:NT, :]).then_inc(x_in2, 16)
            sp.dma_start(tab[:, :], tables).then_inc(tab_in, 16)
            sp.dma_start(small[:, :], w_small).then_inc(small_in, 16)
            sp.dma_start(tab16[:, :], tables16).then_inc(tab_in, 16)
            hj = NT // 2

            def load_adj(i, slot):
                for k in range(2):
                    sp.dma_start(adj2[:, slot, k * hj:(k + 1) * hj, :],
                                 adj[i, :, k * hj:(k + 1) * hj, :]).then_inc(adj_in[k], 16)
            load_adj(0, 0)
            for k in range(2):
                sp.wait_ge(adj_in[k], 16)
            load_adj(1, 1)
            for i in range(2, NB):
                sp.wait_ge(g_masked, RING + NT * (i - 1))
                for k in range(2):
                    sp.wait_ge(adj_in[k], 16 * i)
                load_adj(i, i % 2)
            sp.wait_ge(g_masked, RING + NT * NB)
            sp.dma_start(rope_f, rope).then_inc(rope_in, 16)
            for part, (b0, b1) in enumerate(STACKED):
                sp.wait_ge(ql_done, b1)
                sp.wait_ge(qh_done, b1)
                for h in range(NH):
                    for row, half in ((1, QKh), (2, QKh), (3, QKl)):
                        sp.dma_start(Qs[32 * row:32 * row + 32, b0:b1, h, :],
                                     half[HD * h:HD * h + HD, 0, b0 * BT:b1 * BT]
                                     .rearrange("p (b t) -> p b t", t=BT)).then_inc(stacks_in[part], 16)
                for g in range(NKV):
                    for row, half in ((1, QKh), (2, QKl), (3, QKh)):
                        sp.dma_start(Ks[32 * row:32 * row + 32, g, b0 * BT:b1 * BT],
                                     half[HD * g:HD * g + HD, 1, b0 * BT:b1 * BT]).then_inc(stacks_in[part], 16)
            for part in range(len(STACKED)):
                sp.wait_ge(stacks_in[part], 16 * STACKS)
            sp.dma_start(W1f, w1).then_inc(w_in, 16)
            sp.dma_start(W3f, w3).then_inc(w_in, 16)
            sp.wait_ge(wl_done, 2)
            sp.wait_ge(wh_done, 2)
            sp.dma_start(W2f, w2).then_inc(w2_in, 16)
            for n, (b0, b1) in enumerate(STORED):
                sp.wait_ge(acc_done, (NE - 2) * NB + 2 * b1)
                sp.dma_start(out[:, 2 * b0:2 * b1, :], U[:, 2 * b0:2 * b1, :]).then_inc(stored, 16)
            sp.wait_ge(stored, 16 * len(STORED))

        @block.gpsimd
        def _(pool):
            pool.memset(H1[:, :, C:C + 1], 1.0).then_inc(filled, 1)
            pool.memset(zero16[:, :], 0.0).then_inc(filled, 1)
            pool.memset(bias[:, 0:1], LN_EPS).then_inc(filled, 1)
            pool.memset(bias[:, 1:2], RMS_EPS).then_inc(filled, 1)
            pool.memset(V16[:, :, :, HD:HD + 1], 1.0).then_inc(filled, 1)

            pool.memset(Ks[0:32, :, :], 0.0).then_inc(pool_step, 1)
            pool.wait_ge(pool_step, 1)
            pool.memset(Ks[0:NH, :, :], 1.0).then_inc(filled, 1)

            pool.memset(Qs[0:32, :, :, :], 0.0).then_inc(filled, 1)

            def rope_add(i):
                pool.wait_ge(rope_parts, i + 1)
                wait(pool, qh_done, i)
                pool.tensor_tensor(qr, ra, rb, ALU.add).then_inc(rope_sum, 1)

            def q_low(i):
                pool.wait_ge(qh_done, i + 1)
                pool.tensor_tensor(QKl[:, :, bass.ts(i, BT)], qr.rearrange("p (a t) -> p a t", a=2),
                                   QKh[:, :, bass.ts(i, BT)], ALU.subtract).then_inc(ql_done, 1)
                pool.wait_ge(ql_done, i + 1)
            skewed(pool, NB, [(1, q_low), (0, rope_add)])

            n_e = Count(pool, "tiles_e", 1 + RING)

            def e_low_pair():
                for u in range(2):
                    pool.wait_ge(e_ready, n_e.now())
                    pool.tensor_tensor(EL[u][:, 0:PC], E[u][:, 0:PC], EH[u][:, 0:PC],
                                       ALU.subtract).then_inc(el_pool, 1)
                    n_e.up()

            pool.sem_inc(el_pool, RING)
            e_low_pair()
            with pool.Fori(1, W13_BLOCK) as i:
                with pool.Fori(0, i + 1):
                    e_low_pair()
            for k, (full, high, low) in enumerate(((W1f, W1h, W1l), (W3f, W3h, W3l))):
                pool.wait_ge(wh_done, k + 1)
                pool.tensor_tensor(low, full, high, ALU.subtract).then_inc(wl_done, 1)
            with pool.Fori(W13_BLOCK, NB - 1) as i:
                with pool.Fori(0, i + 1):
                    e_low_pair()
            pool.wait_ge(wh_done, 3)
            pool.tensor_tensor(W2l, W2f, W2h, ALU.subtract).then_inc(wl_done, 1)
            with pool.Fori(0, NB):
                e_low_pair()

            def f_low(i):
                pool.wait_ge(fh_done, i + 1)
                pool.tensor_tensor(F16l[:, bass.ts(i, BT)], tb[:, :], F16h[:, bass.ts(i, BT)],
                                   ALU.subtract).then_inc(fl_done, 1)
            skewed(pool, NB, [(0, f_low)])

            def gated_rest(m, u):
                pool.wait_ge(gated_high, m + 1)
                wait(pool, y_done, m - 1)
                pool.tensor_tensor(hhl[u], hh_[u], hhh[u], ALU.subtract).then_inc(gated_low, 1)
            for u in range(2):
                gated_rest(u, u)
            with pool.Fori(1, NE // 2 * NB) as k:
                for u in range(2):
                    gated_rest(k * 2 + u, u)

        @block.scalar
        def _(act):
            def roots(n, eps):
                act.wait_ge(rt_ask, n)
                act.activation(stat[:, 2, :], stat[:, 1, :], ACT.Sqrt, bias=bias[:, eps:eps + 1]).then_inc(rt_done, 1)

            act.wait_ge(filled, 5)
            roots(1, 0)

            def turned_copy(i):
                act.wait_ge(turned, i + 1)
                wait(act, qk_done, i)
                act.activation(tb[:, :], ps[:, 0, 0:BT], ACT.Copy).then_inc(turned_read, 1)
                act.activation(H1[:, bass.ts(i, 2), 0:C], nb_[:, :, :], ACT.Copy).then_inc(h_kept, 1)

            def qk_square(i):
                act.wait_ge(qk_done, i + 1)
                wait(act, sums_done, i)
                act.activation(sq, nat(i), ACT.Square).then_inc(qk_squared, 1)

            def qk_root(i):
                act.wait_ge(sums_done, i + 1)
                wait(act, qn_done, i)
                act.activation(ss4[:, 1, :], ss4[:, 0, :], ACT.Sqrt).then_inc(roots_done, 1)

            def qk_high(i):
                act.wait_ge(qn_turned, i + 1)
                act.activation(QKh[:, :, bass.ts(i, BT)], ps[:, 3, :].rearrange("p (a t) -> p a t", a=2),
                               ACT.Copy).then_inc(qkh_done, 1)
            skewed(act, NB, [(3, qk_high), (2, qk_root), (1, qk_square), (0, turned_copy)])

            def g_exps(m, u):
                act.wait_ge(g_scored, m + 1)
                act.wait_ge(g_masked, m + 1)
                act.activation(Eg[u], ps[:, u, 0:BT], ACT.Exp, scale=1.0 / (UNIT * UNIT)).then_inc(g_exp, 1)

            def load_table(func):
                act.activation(unused[:, :], bias[:, 0:1], func).then_inc(table_in, 1)
            load_table(ACT.Exp)
            act.sem_inc(g_exp, RING)
            with act.Fori(0, NB * NB) as k:
                for u in range(2):
                    g_exps(k * 2 + u, u)

            roots(2, 0)
            roots(3, 1)

            def q_turned(i):
                act.wait_ge(turned, P2N + i + 1)
                wait(act, proj_done, i)
                act.activation(tb[:, :], ps[:, 0, 0:BT], ACT.Copy, scale=ln1).then_inc(turned_read, 1)

            def v_high(i):
                act.wait_ge(proj_done, i + 1)
                act.activation(V16[:, bass.ts(i, 2), :, 0:HD], v_bank(i), ACT.Copy).then_inc(vh_done, 1)

            def q_high(i):
                act.wait_ge(rope_sum, i + 1)
                act.activation(QKh[:, :, bass.ts(i, BT)], qr.rearrange("p (a t) -> p a t", a=2),
                               ACT.Copy).then_inc(qh_done, 1)
            skewed(act, NB, [(1, v_high), (1, q_high), (0, q_turned)])

            load_table(ACT.Exp)
            n = Count(act, "act_tiles", 1)
            done = Count(act, "act_used", 0)

            def exp_pair():
                for u in range(2):
                    pair_of_banks = ps[:, 2 + 2 * u:4 + 2 * u, :].rearrange("p a c -> p (a c)")
                    act.wait_ge(s_ready, n.now())
                    act.wait_ge(el_pool, n.now())
                    act.wait_ge(el_dve, n.now())
                    act.activation(E[u], pair_of_banks, ACT.Exp, scale=SCALE).then_inc(e_full, 1)
                    act.wait_ge(pv_done, n.now())
                    act.activation(EH[u], pair_of_banks, ACT.Exp, scale=SCALE).then_inc(e_ready, 1)
                    n.up()
                done.up(2)

            def out_copy():
                act.wait_ge(pv_done, done.now())
                act.activation(OT[0:VW, :, :], ps[0:VW, 6:8, :], ACT.Copy).then_inc(ot_ready, 1)

            def attention_exps(i):
                exp_pair()
                out_copy()
                with act.Fori(0, i):
                    exp_pair()

            act.sem_inc(e_ready, RING)
            act.sem_inc(pv_done, RING)
            exp_pair()
            with act.Fori(1, W13_BLOCK) as i:
                attention_exps(i)
            act.wait_ge(w_in, 32)
            act.activation(W1h, W1f, ACT.Copy).then_inc(wh_done, 1)
            act.activation(W3h, W3f, ACT.Copy).then_inc(wh_done, 1)
            with act.Fori(W13_BLOCK, NB - 1) as i:
                attention_exps(i)
            act.wait_ge(w2_in, 16)
            act.activation(W2h, W2f, ACT.Copy).then_inc(wh_done, 1)
            attention_exps(NB - 1)
            done.up(2)
            out_copy()

            roots(4, 1)

            def f_turned(i):
                act.wait_ge(turned, P4N + i + 1)
                wait(act, lg_done, i)
                wait(act, fl_done, i)
                act.activation(tb[:, :], ps[:, 0, 0:BT], ACT.Copy, scale=ln2).then_inc(turned_read, 1)

            def keep_logits(i):
                act.wait_ge(lg_done, i + 1)
                act.activation(LG[:, bass.ts(i, 2), :], ps[:, 1, 0:2 * NE].rearrange("p (t e) -> p t e", t=2),
                               ACT.Copy).then_inc(lg_kept, 1)
            skewed(act, NB, [(1, keep_logits), (0, f_turned)])

            act.wait_ge(gate_ready, 1)
            act.activation(R[1][:, :, :], R[0][:, :, :], ACT.Exp).then_inc(act_step, 1)

            def silu(m, u):
                act.wait_ge(hid_done, m + 1)
                act.wait_ge(gated, m + 1)
                act.activation(sl[u], hidden(u)[:, 0:HC * BT], ACT.Silu).then_inc(silu_done, 1)

            def gated_highs(m, u):
                act.wait_ge(gated, m + 1 + RING)
                wait(act, y_done, m - 1)
                act.activation(hhh[u], hh_[u], ACT.Copy).then_inc(gated_high, 1)
            load_table(ACT.Silu)
            silu(0, 0)
            silu(1, 1)
            gated_highs(0, 0)
            silu(2, 0)
            gated_highs(1, 1)
            with act.Fori(1, NE // 2 * NB - 1) as k:
                silu(k * 2 + 1, 1)
                gated_highs(k * 2, 0)
                silu(k * 2 + 2, 0)
                gated_highs(k * 2 + 1, 1)
            m = NE * NB - 2
            silu(m + 1, 1)
            gated_highs(m, 0)
            gated_highs(m + 1, 1)

        @block.vector
        def _(dve):
            own = Count(dve, "own", 0)

            def link(ins):
                ins.then_inc(dve_step, 1)
                own.up()
                dve.wait_ge(dve_step, own.now())

            def tile_of(v, i, t):
                return v[:, bass.ds(i * 2 + t, 1), :].rearrange("p a c -> p (a c)")

            def row_moments(mean, var):
                me, mo, ve, vo = (st6[:, :, k] for k in (1, 4, 2, 5))
                link(dve.tensor_tensor(mean, me, mo, ALU.add))
                link(dve.tensor_scalar(mean, mean, 0.5, None, ALU.mult))
                link(dve.tensor_tensor(stat[:, 6, :], me, mo, ALU.subtract))
                link(dve.scalar_tensor_tensor(out=stat[:, 6, :], in0=stat[:, 6, :], scalar=0.25,
                                              in1=stat[:, 6, :], op0=ALU.mult, op1=ALU.mult))
                link(dve.tensor_tensor(stat[:, 7, :], ve, vo, ALU.add))
                link(dve.scalar_tensor_tensor(out=var, in0=stat[:, 7, :], scalar=1.0 / C, in1=stat[:, 6, :],
                                              op0=ALU.mult, op1=ALU.add))

            def one_over_root(n, dst):
                dve.sem_inc(rt_ask, 1)
                dve.wait_ge(rt_done, n)
                link(dve.reciprocal(dst, stat[:, 2, :]))

            MEAN, VAR, RSTD, RBOTH = stat[:, 0, :], stat[:, 1, :], stat[:, 3, :], stat[:, 4, :]

            def layernormed(dst, i, t, scale):
                return dve.tensor_scalar(dst, tile_of(X1, i, t), MEAN[:, bass.ds(i * 2 + t, 1)],
                                         scale[:, bass.ds(i * 2 + t, 1)], ALU.subtract, ALU.mult)

            with dve.Fori(0, NB // 2) as i:
                dve.wait_ge(x_in, 16)
                for t in range(2):
                    dve.bn_stats(st6[:, bass.ds(i * 2 + t, 1), :].rearrange("p a c -> p (a c)"),
                                 tile_of(X1, i, t)).then_inc(stats_done, 1)
            with dve.Fori(NB // 2, NB) as i:
                dve.wait_ge(x_in, 16)
                dve.wait_ge(x_in2, 16)
                for t in range(2):
                    dve.bn_stats(st6[:, bass.ds(i * 2 + t, 1), :].rearrange("p a c -> p (a c)"),
                                 tile_of(X1, i, t)).then_inc(stats_done, 1)
            dve.wait_ge(stats_done, NT)
            row_moments(MEAN, VAR)
            one_over_root(1, RSTD)

            def normalized(i):
                wait(dve, turned, i)
                wait(dve, h_kept, i)
                for t in range(2):
                    ins = layernormed(nb_[:, t, :], i, t, RSTD)
                ins.then_inc(norm_ready, 1)

            def qk_sums(i):
                dve.wait_ge(qk_squared, i + 1)
                dve.tensor_reduce(ss4[:, 0, :], sq.rearrange("p (a c) -> p a c", a=4), X, ALU.add
                                  ).then_inc(sums_done, 1)

            def qk_norm(i):
                dve.wait_ge(roots_done, i + 1)
                wait(dve, qn_turned, i)
                link(dve.tensor_scalar(ss4[:, 1, :], ss4[:, 1, :], COS_EPS, 1.0 / UNIT, ALU.max, ALU.mult))
                link(dve.reciprocal(ss4[:, 1, :], ss4[:, 1, :]))
                dve.tensor_tensor(qn.rearrange("p (a c) -> p a c", a=4),
                                  nat(i).rearrange("p (a c) -> p a c", a=4),
                                  rows(ss4[:, 1, :], C), ALU.mult).then_inc(qn_done, 1)

            def qk_low(i):
                dve.wait_ge(qkh_done, i + 1)
                dve.tensor_tensor(QKl[:, :, bass.ts(i, BT)], ps[:, 3, :].rearrange("p (a t) -> p a t", a=2),
                                  QKh[:, :, bass.ts(i, BT)], ALU.subtract).then_inc(qkl_done, 1)
            skewed(dve, NB, [(3, qk_low), (2, qk_norm), (0, normalized), (1, qk_sums)])

            def mask(m, u, adj_tile):
                dve.wait_ge(g_exp, m + 1 + RING)
                wait(dve, g_prop, m - 1)
                dve.scalar_tensor_tensor(out=Em[u], in0=adj_tile, scalar=0.0, in1=Eg[u],
                                         op0=ALU.is_gt, op1=ALU.mult).then_inc(g_masked, 1)

            def adj_tile(slot, jt):
                return adj2[:, bass.ds(slot, 1), bass.ds(jt, 1), :].rearrange("p a b c -> p (a b c)")

            has, inv, keep = gs[:, 0:2], gs[:, 2:4], gs[:, 4:6]

            def g_result(i):
                return ps[:, bass.ds(4 + i % 2, 1), :].rearrange("p a c -> p (a c)")[:, 0:2 * (C + 1)] \
                    .rearrange("p (t c) -> p t c", t=2)

            def sums_of(i):
                return g_result(i)[:, :, C:C + 1].rearrange("p t c -> p (t c)")

            def shares_1(i):
                dve.wait_ge(g_prop, NT * (i + 1))
                link(dve.tensor_scalar(has, sums_of(i), 0.0, None, ALU.is_gt))
                link(dve.scalar_tensor_tensor(out=inv, in0=sums_of(i), scalar=1.0, in1=has, op0=ALU.add,
                                              op1=ALU.subtract))

            def shares_2(i):
                link(dve.reciprocal(inv, inv))
                link(dve.scalar_tensor_tensor(out=inv, in0=inv, scalar=0.5, in1=has, op0=ALU.mult, op1=ALU.mult))
                link(dve.tensor_scalar(keep, has, -0.5, 1.0, ALU.mult, ALU.add))

            def blend_1(i, t):
                link(dve.scalar_tensor_tensor(out=gt[:, t, :], in0=g_result(i)[:, t, 0:C], scalar=inv[:, t:t + 1],
                                              in1=tile_of(X1, i, t), op0=ALU.mult, op1=ALU.add))

            def blend_2(i, t):
                dve.scalar_tensor_tensor(
                    out=tile_of(X1, i, t), in0=H1[:, bass.ds(i * 2 + t, 1), 0:C].rearrange("p a c -> p (a c)"),
                    scalar=keep[:, t:t + 1], in1=gt[:, t, :], op0=ALU.mult, op1=ALU.add).then_inc(x1_done, 1)

            def x1_moments(i):
                dve.wait_ge(x1_done, (i + 1) * 2)
                for t in range(2):
                    dve.bn_stats(st6[:, bass.ds(i * 2 + t, 1), :].rearrange("p a c -> p (a c)"),
                                 tile_of(X1, i, t)).then_inc(stats_done, 1)

            dve.sem_inc(g_masked, RING)
            for k in range(2):
                dve.wait_ge(adj_in[k], 16)
            for u in range(2):
                mask(u, u, adj_tile(0, u))
            with dve.Fori(1, NB) as j:
                for u in range(2):
                    mask(j * 2 + u, u, adj_tile(0, j * 2 + u))
            with dve.Fori(1, NB) as i:
                slot = dve.snap(i % 2)
                for k in range(2):
                    dve.wait_ge(adj_in[k], 16 * (i + 1))
                m0 = i * NT
                mask(m0, 0, adj_tile(slot, 0))
                mask(m0 + 1, 1, adj_tile(slot, 1))
                shares_1(i - 1)
                mask(m0 + 2, 0, adj_tile(slot, 2))
                shares_2(i - 1)
                mask(m0 + 3, 1, adj_tile(slot, 3))
                blend_1(i - 1, 0)
                mask(m0 + 4, 0, adj_tile(slot, 4))
                blend_2(i - 1, 0)
                blend_1(i - 1, 1)
                mask(m0 + 5, 1, adj_tile(slot, 5))
                blend_2(i - 1, 1)
                mask(m0 + 6, 0, adj_tile(slot, 6))
                x1_moments(i - 1)
                mask(m0 + 7, 1, adj_tile(slot, 7))
                with dve.Fori(4, NB) as j:
                    for u in range(2):
                        mask(m0 + j * 2 + u, u, adj_tile(slot, j * 2 + u))
            shares_1(NB - 1)
            shares_2(NB - 1)
            for t in range(2):
                blend_1(NB - 1, t)
                blend_2(NB - 1, t)
            x1_moments(NB - 1)

            dve.wait_ge(stats_done, 2 * NT)
            row_moments(MEAN, VAR)
            one_over_root(2, RSTD)
            link(dve.tensor_tensor(VAR, VAR, RSTD, ALU.mult))
            link(dve.tensor_tensor(VAR, VAR, RSTD, ALU.mult))
            one_over_root(3, RBOTH)
            link(dve.tensor_tensor(RBOTH, RBOTH, RSTD, ALU.mult))

            def both_normalized(i):
                wait(dve, turned, P2N + i)
                for t in range(2):
                    ins = layernormed(nb_[:, t, :], i, t, RBOTH)
                ins.then_inc(norm_ready, 1)
                for t in range(2):
                    layernormed(tile_of(U, i, t), i, t, RSTD).then_inc(u_done, 1)

            def rope_halves(i):
                dve.wait_ge(proj_done, i + 1)
                wait(dve, rope_sum, i)
                for k, dst in ((0, ra), (1, rb)):
                    ins = dve.tensor_tensor(dst.rearrange("p (a t) -> p a t", a=2),
                                            qk_banks(i, k).rearrange("p (a t) -> p a t", a=2),
                                            rope_f[:, k, bass.ts(i, BT)].unsqueeze(1).to_broadcast([P, 2, BT]),
                                            ALU.mult)
                ins.then_inc(rope_parts, 1)

            def v_low(i):
                dve.wait_ge(vh_done, i + 1)
                dve.tensor_tensor(V16[:, bass.ts(i, 2), :, HD + 1:VW], v_bank(i),
                                  V16[:, bass.ts(i, 2), :, 0:HD], ALU.subtract).then_inc(v_done, 1)
            dve.wait_ge(rope_in, 16)
            skewed(dve, NB, [(0, both_normalized), (1, rope_halves), (1, v_low)])

            a = Count(dve, "a", 1)
            a_freed = Count(dve, "a_freed", RING)
            n_e = Count(dve, "tiles_e", 1 + RING)

            def a_bank(s):
                return ps[:, s, :]

            def chunk_max(j, t):
                for g in range(NKV):
                    dve.wait_ge(a_ready, a.now())
                    dve.tensor_reduce(cm[:, t, 2 * g:2 * g + 2, bass.ds(j, 1)].rearrange("p h j -> p (h j)"),
                                      a_bank(g).rearrange("p (h k) -> p h k", h=2), X, ALU.max
                                      ).then_inc(a_free, 1)
                    a.up()
                    a_freed.up()

            def block_max():
                dve.wait_ge(a_free, a_freed.now())
                link(dve.tensor_reduce(m8[:, :, :].rearrange("p t h -> p (t h)"),
                                       cm[:, :, :, :].rearrange("p t h j -> p (t h) j"), X, ALU.max))
                dve.sem_inc(m_ready, 1)
                dve.memset(cm[:, :, :, :], LOWEST).then_inc(dve_step, 1)
                own.up()

            def negated_max(i):
                for t in range(2):
                    dve.wait_ge(a_ready, a.now())
                    dve.tensor_tensor(Qs[0:NH, bass.ds(i, 1), :, t * P:t * P + P].rearrange("p a h t -> p (a h) t"),
                                      a_bank(t)[0:NH, 0:P].unsqueeze(1).to_broadcast([NH, NH, P]),
                                      negblk, ALU.mult).then_inc(a_free, 1)
                    a.up()
                    a_freed.up()
                dve.wait_ge(a_free, a_freed.now())
                dve.sem_inc(negm_done, 1)

            def e_low(u):
                dve.wait_ge(e_ready, n_e.now())
                dve.tensor_tensor(EL[u][:, PC:1024], E[u][:, PC:1024], EH[u][:, PC:1024],
                                  ALU.subtract).then_inc(el_dve, 1)
                n_e.up()

            def attention_out(i, t):
                ut = tile_of(U, i, t)
                for g in range(NKV):
                    dve.wait_ge(a_ready, a.now())
                    z = a_bank(g)[:, 0:2 * (C + 1)].rearrange("p (h c) -> p h c", h=2)
                    link(dve.reciprocal(zr[:, :], z[:, :, C:C + 1].rearrange("p h c -> p (h c)")))
                    link(dve.scalar_tensor_tensor(out=ut, in0=z[:, 0, 0:C], scalar=zr[:, 0:1], in1=ut,
                                                  op0=ALU.mult, op1=ALU.add))
                    link(dve.scalar_tensor_tensor(out=ut, in0=z[:, 1, 0:C], scalar=zr[:, 1:2], in1=ut,
                                                  op0=ALU.mult, op1=ALU.add))
                    dve.sem_inc(a_free, 1)
                    a.up()
                    a_freed.up()
                dve.bn_stats(st6[:, bass.ds(i * 2 + t, 1), :].rearrange("p a c -> p (a c)"),
                             ut).then_inc(stats_done, 1)

            dve.sem_inc(a_free, RING)
            dve.sem_inc(el_dve, RING)
            dve.sem_inc(gated, RING)
            link(dve.memset(cm[:, :, :, :], LOWEST))
            for t in range(2):
                chunk_max(0, t)
            block_max()
            negated_max(0)
            dve.wait_ge(dve_step, own.now())
            for j in (1, 0):
                for t in range(2):
                    chunk_max(j, t)
            block_max()

            def attention_block(i, after=True, negate=True):
                if after:
                    dve.wait_ge(dve_step, own.now())
                    chunk_max(i + 2, 0)
                    chunk_max(i + 2, 1)
                if negate:
                    negated_max(i + 1)
                e_low(0)
                if after:
                    chunk_max(i + 1, 0)
                attention_out(i - 1, 0)
                e_low(1)
                if after:
                    chunk_max(i + 1, 1)
                attention_out(i - 1, 1)
                if after:
                    chunk_max(0, 0)
                e_low(0)
                if after:
                    chunk_max(0, 1)
                def steps(j):
                    for t in range(2):
                        if after:
                            chunk_max(j, t)
                        e_low(1 - t)
                if not (isinstance(i, int) and i == 1):
                    with dve.Fori(1, i) as j:
                        steps(j)
                if after:
                    chunk_max(i, 0)
                    chunk_max(i, 1)
                e_low(1)
                if after:
                    block_max()

            dve.wait_ge(dve_step, own.now())
            chunk_max(2, 0)
            chunk_max(2, 1)
            negated_max(1)
            e_low(0)
            for j in (1, 0):
                chunk_max(j, 0)
                chunk_max(j, 1)
            e_low(1)
            block_max()
            attention_block(1)
            with dve.Fori(2, NB - 2) as i:
                attention_block(i)
            attention_block(NB - 2, after=False)
            attention_block(NB - 1, after=False, negate=False)
            for t in range(2):
                attention_out(NB - 1, t)

            dve.wait_ge(stats_done, 3 * NT)
            row_moments(MEAN, VAR)
            link(dve.tensor_tensor(MEAN, MEAN, MEAN, ALU.mult))
            link(dve.tensor_tensor(VAR, VAR, MEAN, ALU.add))
            one_over_root(4, RSTD)

            def rms_normalized(i):
                wait(dve, turned, P4N + i)
                dve.tensor_tensor(nb_[:, :, :], U[:, bass.ts(i, 2), :],
                                  rows(RSTD[:, bass.ts(i, 2)], C), ALU.mult).then_inc(norm_ready, 1)

            def f_high(i):
                dve.wait_ge(turned_read, P4N + i + 1)
                dve.tensor_copy(F16h[:, bass.ts(i, BT)], tb[:, :]).then_inc(fh_done, 1)
            skewed(dve, NB, [(0, rms_normalized), (1, f_high)])

            dve.wait_ge(lg_kept, NB)
            big, tot, r = rs[:, 0, :], rs[:, 1, :], R
            revb = rev.unsqueeze(1).to_broadcast([P, NT, NE])
            link(dve.tensor_reduce(big, LG[:, :, :], X, ALU.max))
            dve.tensor_tensor(r[0][:, :, :], LG[:, :, :], rows(big, NE), ALU.subtract).then_inc(gate_ready, 1)
            dve.wait_ge(act_step, 1)
            link(dve.tensor_reduce(tot, r[1][:, :, :], X, ALU.add))
            link(dve.reciprocal(tot, tot))
            link(dve.tensor_tensor(r[1][:, :, :], r[1][:, :, :], rows(tot, NE), ALU.mult))

            def first_largest(probs, dst, top, pick):
                link(dve.tensor_reduce(top, probs, X, ALU.max))
                link(dve.tensor_tensor(dst, probs, rows(top, NE), ALU.is_equal))
                link(dve.tensor_tensor(dst, dst, revb, ALU.mult))
                link(dve.tensor_reduce(pick, dst, X, ALU.max))
                link(dve.tensor_tensor(dst, dst, rows(pick, NE), ALU.is_equal))
            first_largest(r[1][:, :, :], r[0][:, :, :], rs[:, 2, :], rs[:, 3, :])
            link(dve.scalar_tensor_tensor(out=r[2][:, :, :].rearrange("p t e -> p (t e)"),
                                          in0=r[0][:, :, :].rearrange("p t e -> p (t e)"), scalar=-2.0,
                                          in1=r[1][:, :, :].rearrange("p t e -> p (t e)"),
                                          op0=ALU.mult, op1=ALU.add))
            first_largest(r[2][:, :, :], r[3][:, :, :], rs[:, 4, :], rs[:, 5, :])
            link(dve.tensor_tensor(r[0][:, :, :], r[0][:, :, :], r[3][:, :, :], ALU.add))
            link(dve.scalar_tensor_tensor(out=tot, in0=rs[:, 2, :], scalar=1e-9, in1=rs[:, 4, :],
                                          op0=ALU.add, op1=ALU.add))
            link(dve.reciprocal(tot, tot))
            link(dve.tensor_tensor(r[0][:, :, :], r[0][:, :, :], r[1][:, :, :], ALU.mult))
            link(dve.tensor_tensor(GW[:, :, :], r[0][:, :, :], rows(tot, NE), ALU.mult))
            link(dve.tensor_tensor(U[:, :, :], U[:, :, :], X1[:, :, :], ALU.add))

            def gate(m, u):
                dve.wait_ge(silu_done, m + 1)
                wait(dve, gated_low, m - 1)
                dve.tensor_tensor(hh_[u], hidden(u)[:, HC * BT:2 * HC * BT], sl[u], ALU.mult).then_inc(gated, 1)

            def add_expert(m, e, i, u):
                dve.wait_ge(y_done, m + 1)
                wait(dve, acc_done, m)
                for t in range(2):
                    ut = U[:, bass.ds(i * 2 + t, 1), :].rearrange("p a c -> p (a c)")
                    ins = dve.scalar_tensor_tensor(
                        out=ut, in0=ps[:, 6 + u, t * C:(t + 1) * C],
                        scalar=GW[:, bass.ds(i * 2 + t, 1), bass.ds(e, 1)].rearrange("p a c -> p (a c)"),
                        in1=ut, op0=ALU.mult, op1=ALU.add)
                ins.then_inc(acc_done, 1)

            def expert_turn(e2, i, nxt):
                m = e2 * (2 * NB) + i * 2
                for u in range(2):
                    if nxt:
                        gate(m + 2 + u, u)
                    add_expert(m + u, e2 * 2 + u, i, u)

            gate(0, 0)
            gate(1, 1)
            expert_turn(0, 0, True)
            with dve.Fori(1, NB) as i:
                expert_turn(0, i, True)
            with dve.Fori(1, NE // 2 - 1) as e2:
                with dve.Fori(0, NB) as i:
                    expert_turn(e2, i, True)
            with dve.Fori(0, NB - 1) as i:
                expert_turn(NE // 2 - 1, i, True)
            expert_turn(NE // 2 - 1, NB - 1, False)

        @block.tensor
        def _(pe):
            def turn(n):
                pe.wait_ge(norm_ready, n + 1)
                wait(pe, turned_read, n)
                for t in range(2):
                    ins = pe.transpose(ps[:, 0, t * P:(t + 1) * P], nb_[:, t, :], ident)
                ins.then_inc(turned, 1)

            pe.wait_ge(tab_in, 32)
            pe.wait_ge(small_in, 16)
            pe.wait_ge(filled, 5)

            def qk(i):
                pe.wait_ge(turned_read, i + 1)
                wait(pe, qn_done, i - 1)
                for t in range(2):
                    ins = pe.matmul(nat(i)[:, t * 2 * C:(t + 1) * 2 * C], tb[:, t * P:(t + 1) * P], Wqk,
                                    start=True, stop=True)
                ins.then_inc(qk_done, 1)

            def qk_turn(i):
                pe.wait_ge(qn_done, i + 1)
                wait(pe, qkl_done, i)
                for t in range(2):
                    for k in range(2):
                        ins = pe.transpose(ps[:, 3, k * BT + t * P:k * BT + (t + 1) * P],
                                           qn[:, (2 * t + k) * C:(2 * t + k + 1) * C], ident)
                ins.then_inc(qn_turned, 1)
            skewed(pe, NB, [(3, qk_turn), (1, qk), (0, turn)])

            def g_scores(i, jt, u, m):
                pe.wait_ge(g_exp, m + 1)
                parts = ((QKh, QKh), (QKh, QKl), (QKl, QKh))
                for k, (qa, ka) in enumerate(parts):
                    ins = pe.matmul(ps[:, u, 0:BT], qa[:, 0, bass.ts(jt, P)], ka[:, 1, bass.ts(i, BT)],
                                    start=(k == 0), stop=(k == len(parts) - 1))
                ins.then_inc(g_scored, 1)

            def g_bank(slot):
                return ps[:, bass.ds(4 + slot, 1), :].rearrange("p a c -> p (a c)")

            def g_clear(i, slot):
                wait(pe, x1_done, (i - 1) * 2)
                pe.matmul(g_bank(slot)[:, 0:2 * (C + 1)], zero16[:, 0:P], zero16[:, 0:2 * (C + 1)],
                          start=True, stop=False, skip_group_check=True)

            def g_propagate(slot, jt, u, m):
                pe.wait_ge(g_masked, m + 1 + RING)
                for t in range(2):
                    ins = pe.matmul(g_bank(slot)[:, t * (C + 1):(t + 1) * (C + 1)], Em[u][:, t * P:(t + 1) * P],
                                    H1[:, bass.ds(jt, 1), :].rearrange("p a c -> p (a c)"),
                                    start=False, stop=False, skip_group_check=True)
                ins.then_inc(g_prop, 1)

            def g_block(i, nxt):
                slot = i % 2 if isinstance(i, int) else pe.snap(i % 2)
                g_clear(i, slot)
                with pe.Fori(0, NB - 1) as j:
                    for u in range(2):
                        m = i * NT + j * 2 + u
                        g_scores(i, j * 2 + 2 + u, u, m + 2)
                        g_propagate(slot, j * 2 + u, u, m)
                for u in range(2):
                    m = i * NT + NT - 2 + u
                    if nxt:
                        g_scores(i + 1, u, u, m + 2)
                    g_propagate(slot, NT - 2 + u, u, m)

            pe.wait_ge(qkl_done, NB)
            pe.wait_ge(h_kept, NB)
            for u in range(2):
                g_scores(0, u, u, u)
            g_block(0, True)
            g_block(1, True)
            with pe.Fori(2, NB - 1) as i:
                g_block(i, True)
            g_block(NB - 1, False)

            def project(i):
                pe.wait_ge(turned_read, P2N + i + 1)
                wait(pe, rope_parts, i - 1)
                wait(pe, v_done, i - 1)
                for k in range(4):
                    pe.matmul(qk_banks(i, k // 2)[:, (k % 2) * BT:(k % 2 + 1) * BT], Wf[:, k * P:(k + 1) * P], tb[:, :],
                              start=True, stop=True)
                for t in range(2):
                    ins = pe.matmul(v_bank(i)[:, t, :, :].rearrange("p g d -> p (g d)"), tb[:, t * P:(t + 1) * P], Wv,
                                    start=True, stop=True)
                ins.then_inc(proj_done, 1)
            skewed(pe, NB, [(1, project), (0, lambda i: turn(P2N + i))])

            pe.wait_ge(stacks_in[0], 16 * STACKS)
            pe.wait_ge(filled, 7)
            pe.wait_ge(rope_parts, NB)
            pe.wait_ge(v_done, NB)
            a = Count(pe, "a_slot", 1)
            s = Count(pe, "s_slot", 1)
            v = Count(pe, "v_tile", 1 + RING)

            def a_task(u, fill):
                pe.wait_ge(a_free, a.now())
                fill(ps[:, u, :]).then_inc(a_ready, 1)
                a.up()

            def row_chunk(i, j, t, diagonal=False):
                for g in range(NKV):
                    def fill(bank):
                        if diagonal:
                            pe.matmul(bank, ident16, maskA[:, t, :], start=True, stop=False,
                                      skip_group_check=True)
                        for h in range(2):
                            ins = pe.matmul(bank[:, h * BT:(h + 1) * BT],
                                            Qs[:, bass.ds(i, 1), 2 * g + h, t * P:(t + 1) * P]
                                            .rearrange("p a t -> p (a t)"),
                                            Ks[:, g, bass.ts(j, BT)], start=not diagonal, stop=True,
                                            skip_group_check=True)
                        return ins
                    a_task(g, fill)

            def maxima(i):
                pe.wait_ge(m_ready, i + 1)
                for t in range(2):
                    a_task(t, lambda bank: pe.transpose(bank[0:NH, 0:P], m8[:, t, :], ident))

            def scores(i, j, u, diagonal=False):
                pe.wait_ge(e_ready, s.now())
                for g in range(NKV):
                    bank = ps[:, 2 + 2 * u + g, :]
                    ins = pe.matmul(bank, Ks[:, g, bass.ts(j * 2 + u, P)],
                                    Qs[:, bass.ds(i, 1), 2 * g:2 * g + 2, :].rearrange("p a h t -> p (a h t)"),
                                    start=True, stop=not diagonal)
                    if diagonal:
                        ins = pe.matmul(bank, ident16, maskB[:, u, :], start=False, stop=True)
                ins.then_inc(s_ready, 1)
                s.up()

            def values(j, u, first=False):
                pe.wait_ge(el_pool, v.now())
                pe.wait_ge(el_dve, v.now())
                for part in (EH, EL):
                    for g in range(NKV):
                        ins = pe.matmul(ps[0:VW, 6 + g, :],
                                        V16[:, bass.ds(j * 2 + u, 1), g, :].rearrange("p a c -> p (a c)"),
                                        part[u][:, g * 512:(g + 1) * 512], start=first and part is EH, stop=False,
                                        skip_group_check=True)
                ins.then_inc(pv_done, 1)
                v.up()

            def through_wo(t):
                for g in range(NKV):
                    def fill(bank):
                        for h in range(2):
                            ins = pe.matmul(bank[:, h * (C + 1):(h + 1) * (C + 1)],
                                            OT[0:VW, g, h * BT + t * P:h * BT + (t + 1) * P],
                                            WoA[:, 2 * g + h, :], start=True, stop=True)
                        return ins
                    a_task(g, fill)

            def attention_block(i, after=True, negate=True):
                second = isinstance(i, int) and i == 1
                last = 0 if second else i - 2
                pe.wait_ge(negm_done, i + 1)
                scores(i, i, 0, diagonal=True)
                if after:
                    row_chunk(i + 2, i + 2, 0, diagonal=True)
                values(last, 0, first=second)
                scores(i, i, 1, diagonal=True)
                if after:
                    row_chunk(i + 2, i + 2, 1, diagonal=True)
                values(last, 1)
                scores(i, 0, 0)
                if negate:
                    maxima(i + 1)
                if after:
                    row_chunk(i + 2, i + 1, 0)
                pe.wait_ge(ot_ready, i)
                through_wo(0)
                values(i, 0, first=True)
                scores(i, 0, 1)
                if after:
                    row_chunk(i + 2, i + 1, 1)
                through_wo(1)
                if after:
                    row_chunk(i + 2, 0, 0)
                values(i, 1)
                if after:
                    row_chunk(i + 2, 0, 1)
                if not second:
                    with pe.Fori(1, i) as j:
                        for u in range(2):
                            scores(i, j, u)
                            if after:
                                row_chunk(i + 2, j, u)
                            values(j - 1, u)
                if after:
                    for t in range(2):
                        row_chunk(i + 2, i, t)

            for t in range(2):
                row_chunk(0, 0, t, diagonal=True)
            maxima(0)
            for j in (1, 0):
                for t in range(2):
                    row_chunk(1, j, t, diagonal=j == 1)
            pe.wait_ge(negm_done, 1)
            for u in range(2):
                scores(0, 0, u, diagonal=True)
            for t in range(2):
                row_chunk(2, 2, t, diagonal=True)
            maxima(1)
            for j in (1, 0):
                for t in range(2):
                    row_chunk(2, j, t)
            attention_block(1)
            with pe.Fori(2, NB - 2) as i:
                pe.wait_ge(stacks_in[1], 16 * STACKS)
                attention_block(i)
            attention_block(NB - 2, after=False)
            attention_block(NB - 1, after=False, negate=False)
            for u in range(2):
                values(NB - 2, u)
            pe.wait_ge(ot_ready, NB)
            for t in range(2):
                through_wo(t)

            def route(i):
                pe.wait_ge(turned_read, P4N + i + 1)
                wait(pe, lg_kept, i)
                for t in range(2):
                    ins = pe.matmul(ps[:, 1, t * NE:(t + 1) * NE], tb[:, t * P:(t + 1) * P], Wr,
                                    start=True, stop=True)
                ins.then_inc(lg_done, 1)
            skewed(pe, NB, [(1, route), (0, lambda i: turn(P4N + i))])

            pe.wait_ge(fl_done, NB)
            pe.wait_ge(fh_done, NB)
            pe.wait_ge(wl_done, 3)
            pe.wait_ge(lg_kept, NB)

            def hidden_rows(m, e, i, u):
                pe.wait_ge(gated, m + 1)
                for k, (wh, wl) in enumerate(((W1h, W1l), (W3h, W3l))):
                    for c in range(HC):
                        dst = hidden(u)[:, (k * HC + c) * BT:(k * HC + c + 1) * BT]
                        parts = ((wh, F16h), (wh, F16l), (wl, F16h))
                        for q, (wa, fa) in enumerate(parts):
                            ins = pe.matmul(dst, wa[:, bass.ds(e * HW + c * P, P)], fa[:, bass.ts(i, BT)],
                                            start=(q == 0), stop=(q == len(parts) - 1))
                ins.then_inc(hid_done, 1)

            def expert_out(m, e, u):
                pe.wait_ge(gated_low, m + 1)
                wait(pe, acc_done, m - 1)
                for t in range(2):
                    for c in range(HC):
                        parts = ((hhh, W2h), (hhh, W2l), (hhl, W2h))
                        for q, (ha, wa) in enumerate(parts):
                            ins = pe.matmul(ps[:, 6 + u, t * C:(t + 1) * C],
                                            ha[u][:, c * BT + t * P:c * BT + (t + 1) * P],
                                            wa[:, bass.ds((e * HC + c) * C, C)],
                                            start=(c == 0 and q == 0), stop=(c == HC - 1 and q == len(parts) - 1))
                ins.then_inc(y_done, 1)

            def expert_turn(e2, i, nxt):
                m = e2 * (2 * NB) + i * 2
                for u in range(2):
                    if nxt:
                        hidden_rows(m + 2 + u, nxt[0] * 2 + u, nxt[1], u)
                    expert_out(m + u, e2 * 2 + u, u)

            hidden_rows(0, 0, 0, 0)
            hidden_rows(1, 1, 0, 1)
            expert_turn(0, 0, (0, 1))
            with pe.Fori(1, NB - 1) as i:
                expert_turn(0, i, (0, i + 1))
            expert_turn(0, NB - 1, (1, 0))
            with pe.Fori(1, NE // 2 - 1) as e2:
                with pe.Fori(0, NB - 1) as i:
                    expert_turn(e2, i, (e2, i + 1))
                expert_turn(e2, NB - 1, (e2 + 1, 0))
            with pe.Fori(0, NB - 1) as i:
                expert_turn(NE // 2 - 1, i, (NE // 2 - 1, i + 1))
            expert_turn(NE // 2 - 1, NB - 1, None)


def shape_tables():
    p = np.arange(P)[:, None]
    ident = np.eye(P, dtype=np.float32)
    negblk = np.zeros((P, NH, P), np.float32)
    for h in range(NH):
        negblk[h, h, :] = -1.0
    rev = np.tile(np.arange(NE, 0, -1, dtype=np.float32), (P, 1))
    tables = np.concatenate([ident, np.ones((P, P), np.float32), negblk.reshape(P, -1), rev], axis=1)
    k = np.arange(BT)[None, :]
    mask_a = np.stack([np.tile(np.where(k <= t * P + p, 0.0, FAR), (1, 2)) for t in range(2)], axis=1)
    mask_b = np.stack([np.tile(np.where(k >= t * P + p, 0.0, FAR), (1, 2)) for t in range(2)], axis=1)
    tables16 = np.concatenate([ident, mask_a.reshape(P, -1), mask_b.reshape(P, -1)], axis=1).astype(np.float16)
    inv_freq = 1.0 / 10000.0 ** (np.arange(0, HD, 2, dtype=np.float32) / HD)
    freqs = np.outer(np.arange(TP, dtype=np.float32), inv_freq)
    emb = np.concatenate([freqs, freqs], axis=-1)
    cos, sin = np.cos(emb).T, np.sin(emb).T
    sin = np.concatenate([-sin[:HD // 2], sin[HD // 2:]], axis=0)
    rope = np.stack([np.tile(cos, (P // HD, 1)), np.tile(sin, (P // HD, 1))], axis=1).astype(np.float32)
    return tables, tables16, rope


def kernel(x, adj, L0_gnn_Wq, L0_gnn_Wk, L0_ffn_ln1_w, L0_ffn_ln2_w, L0_ffn_wq, L0_ffn_wk, L0_ffn_wv,
           L0_ffn_wo, L0_ffn_router_w, L0_ffn_w1, L0_ffn_w2, L0_ffn_w3):
    import concourse.bacc as bacc
    from concourse.bass_utils import run_bass_kernel_spmd

    f = lambda v: np.asarray(v)
    tables, tables16, rope = shape_tables()
    pad = TP - NTOK
    xs = np.pad(f(x), ((0, pad), (0, 0))).reshape(NT, P, C).transpose(1, 0, 2)
    adj_t = np.pad(f(adj), ((0, pad), (0, pad))).reshape(NB, BT, NT, P).transpose(0, 3, 2, 1)

    wq, wk, wo = f(L0_ffn_wq), f(L0_ffn_wk), f(L0_ffn_wo)
    partner = lambda w: w.reshape(-1, 2, HD // 2, C)[:, ::-1].reshape(w.shape)
    to_p = lambda w: np.pad(w, ((0, P - w.shape[0]), (0, 0))).T
    wo_aug = np.zeros((P, NH, C + 1), np.float32)
    for h in range(NH):
        head = wo[:, h * HD:(h + 1) * HD].T
        wo_aug[0:HD, h, 0:C] = head
        wo_aug[HD, h, C] = 1.0
        wo_aug[HD + 1:VW, h, 0:C] = head
    w_small = np.concatenate([
        f(L0_gnn_Wq).T, f(L0_gnn_Wk).T, to_p(wq), to_p(wk), to_p(partner(wq)), to_p(partner(wk)),
        f(L0_ffn_wv).T, f(L0_ffn_router_w).T, wo_aug.reshape(P, -1),
        f(L0_ffn_ln1_w)[:, None], f(L0_ffn_ln2_w)[:, None]], axis=1)
    up = lambda w: np.pad(f(w), ((0, 0), (0, HW - HID), (0, 0))).transpose(2, 0, 1).reshape(C, NE * HW)
    down = np.pad(f(L0_ffn_w2), ((0, 0), (0, 0), (0, HW - HID))) \
        .reshape(NE, C, HC, P).transpose(3, 0, 2, 1).reshape(P, NE * HC * C)
    arrays = {"x": xs, "adj": adj_t, "w_small": w_small, "w1": up(L0_ffn_w1), "w3": up(L0_ffn_w3), "w2": down,
              "rope": rope, "tables": tables, "tables16": tables16}
    arrays = {f"in_{k}": np.ascontiguousarray(v) for k, v in arrays.items()}

    nc = bacc.Bacc("TRN2", target_bir_lowering=False, num_devices=1)
    args = [nc.dram_tensor(k, v.shape, mybir.dt.from_np(v.dtype), kind="ExternalInput").ap()
            for k, v in arrays.items()]
    args.append(nc.dram_tensor("out", (P, NT, C), F32, kind="ExternalOutput").ap())
    graph_ffn_program(nc, *args)
    r = run_bass_kernel_spmd(nc, [arrays], core_ids=[0])
    return r.results[0]["out"].transpose(1, 0, 2).reshape(TP, C)[:NTOK]
```

```python
from contextlib import ExitStack

import numpy as np

import concourse.bass as bass
from concourse import mybir

F32 = mybir.dt.float32
F16 = mybir.dt.float16
I32 = mybir.dt.int32
ALU = mybir.AluOpType
ACT = mybir.ActivationFunctionType
X = mybir.AxisListType.X

P = 128
NTOK = 3327
C = 128
NT = -(-NTOK // P)
NB = NT // 2
BT = 2 * P
TP = NT * P
NH, NKV, HD = 4, 2, 32
PC = 704
VW = 2 * HD + 1
NE = 8
HID = int(8 / 3 * C)
HC = -(-HID // P)
HW = HC * P
LN_EPS = 1e-5
RMS_EPS = 1e-6
COS_EPS = 1e-4
UNIT = 64.0
SCALE = float(HD) ** -0.5
FAR = -60000.0
LOWEST = -3.0e38


class Count:

    def __init__(self, eng, name, start):
        self.eng = eng
        self.reg = eng.alloc_register(name)
        eng.reg_mov(self.reg, start)

    def up(self, by=1):
        self.eng.reg_add(self.reg, self.reg, by)

    def now(self):
        return self.reg


def wait(eng, sem, value):
    if isinstance(value, int) and value <= 0:
        return
    eng.wait_ge(sem, value)


def skewed(eng, n, stages):
    most = max(lag for lag, _ in stages)
    lead = most + 2
    for k in range(lead):
        for lag, stage in stages:
            if k >= lag:
                stage(k - lag)
    with eng.Fori(lead, n) as k:
        for lag, stage in stages:
            stage(k - lag)
    for k in range(n, n + most):
        for lag, stage in stages:
            if k - lag < n:
                stage(k - lag)


def graph_ffn_program(nc, x, adj, w_small, w1, w3, w2, rope, tables, tables16, out):
    ctx = ExitStack()
    with ctx:
        def sb(name, shape, dt):
            return ctx.enter_context(nc.sbuf_tensor(name, shape, dt))

        def sem(name):
            return ctx.enter_context(nc.semaphore(name))

        X1 = sb("X1", [P, NT, C], F32)
        H1 = sb("H1", [P, NT, C + 1], F32)
        U = sb("U", [P, NT, C], F32)
        adj_bytes = sb("adj_bytes", [P, 2 * NT * BT], I32)
        half_bytes = sb("half_bytes", [P, 4 * TP], F16)
        Qs = sb("Qs", [P, NB, NH, BT], F16)
        Ks = sb("Ks", [P, NKV, TP], F16)
        V16 = sb("V16", [P, NT, NKV, VW], F16)
        adj2 = adj_bytes[:, :].rearrange("p (s t c) -> p s t c", s=2, t=NT)
        rope_f = adj_bytes[:, 2 * TP:4 * TP].bitcast(F32).rearrange("p (a t) -> p a t", a=2)
        moe_bytes = adj_bytes[:, :].bitcast(F16)
        ew = NE * HW
        W1h, W1l, W3h, W3l = (moe_bytes[:, k * ew:(k + 1) * ew] for k in range(4))
        F16h = moe_bytes[:, 4 * ew:4 * ew + TP]
        F16l = moe_bytes[:, 4 * ew + TP:4 * ew + 2 * TP]
        w2_at = 4 * ew + 2 * TP
        W2h, W2l = (moe_bytes[:, w2_at + k * ew:w2_at + (k + 1) * ew] for k in range(2))
        QKh = half_bytes[:, 0:2 * TP].rearrange("p (a t) -> p a t", a=2)
        QKl = half_bytes[:, 2 * TP:4 * TP].rearrange("p (a t) -> p a t", a=2)
        W1f = half_bytes[:, 0:2 * ew].bitcast(F32)
        W3f = half_bytes[:, 2 * ew:4 * ew].bitcast(F32)
        W2f = W1f

        small = sb("small", [P, w_small.shape[1]], F32)
        at = 0
        def cut(n, rows=P):
            nonlocal at
            at += n
            return small[0:rows, at - n:at]
        Wqk = cut(2 * C)
        Wf = cut(4 * P)
        Wv = cut(NKV * HD)
        Wr = cut(NE)
        WoA = cut(NH * (C + 1), VW).rearrange("p (h c) -> p h c", h=NH)
        ln1 = cut(1)
        ln2 = cut(1)
        tab = sb("tab", [P, tables.shape[1]], F32)
        ident = tab[:, 0:P]
        ones = tab[:, P:2 * P]
        negblk = tab[0:NH, 2 * P:2 * P + NH * P].rearrange("p (h t) -> p h t", h=NH)
        rev = tab[:, 2 * P + NH * P:2 * P + NH * P + NE]
        tab16 = sb("tab16", [P, tables16.shape[1]], F16)
        ident16 = tab16[:, 0:P]
        maskA = tab16[:, P:P + 1024].rearrange("p (t c) -> p t c", t=2)
        maskB = tab16[:, P + 1024:P + 2048].rearrange("p (t c) -> p t c", t=2)
        zero16 = sb("zero16", [P, 512], F16)

        stat = sb("stat", [P, 8, NT], F32)
        bias = sb("bias", [P, 2], F32)
        unused = sb("unused", [P, 8], F32)
        nb_ = sb("nb", [P, 2, C], F32)
        tb = sb("tb", [P, BT], F32)
        tmp = sb("tmp", [P, 4096], F32)
        sq, qn = tmp[:, 0:512], tmp[:, 512:1024]
        ra, rb, qr = tmp[:, 0:512], tmp[:, 512:1024], tmp[:, 1024:1536]
        Eg = [tmp[:, 1024 + 256 * k:1280 + 256 * k] for k in range(2)]
        Em = [tmp[:, 1536 + 256 * k:1792 + 256 * k] for k in range(2)]
        EH = [tmp[:, 512 * k:512 * k + 512].bitcast(F16) for k in range(2)]
        EL = [tmp[:, 1024 + 512 * k:1536 + 512 * k].bitcast(F16) for k in range(2)]
        h_bytes = H1[:, :, :].rearrange("p t c -> p (t c)")
        E = [h_bytes[:, 1024 * k:1024 * k + 1024] for k in range(2)]
        Z = h_bytes[:, 2048:2048 + 8 * (C + 1)].rearrange("p (g t c) -> p g t c", g=NKV, t=2)
        sl = [tmp[:, 768 * k:768 * k + 768] for k in range(2)]
        hh_ = [tmp[:, 1536 + 768 * k:2304 + 768 * k] for k in range(2)]
        hhh = [h_bytes[:, 384 * k:384 * k + 384].bitcast(F16) for k in range(2)]
        hhl = [h_bytes[:, 768 + 384 * k:1152 + 384 * k].bitcast(F16) for k in range(2)]
        st6 = sb("st6", [P, NT, 6], F32)
        ss4 = sb("ss4", [P, 2, 4], F32)
        gs = sb("gs", [P, 8], F32)
        gt = sb("gt", [P, 2, C], F32)
        OT = sb("OT", [P, NKV, 512], F32)
        cm = sb("cm", [P, 2, NH, NB], F32)
        m8 = sb("m8", [P, 2, NH], F32)
        zr = sb("zr", [P, 4], F32)
        LG = sb("LG", [P, NT, NE], F32)
        R = [sb(f"R{k}", [P, NT, NE], F32) for k in range(4)]
        GW = sb("GW", [P, NT, NE], F32)
        rs = sb("rs", [P, 6, NT], F32)

        ps = ctx.enter_context(nc.psum_tensor("ps", [P, 8, 512], F32))

        x_in = [sem(f"x_in{k}") for k in range(4)]
        small_in, tab_in, rope_in, w_in, w2_in = map(sem, (
            "small_in", "tab_in", "rope_in", "w_in", "w2_in"))
        adj_in = [sem("adj_in0"), sem("adj_in1")]
        stacks_in, stored = [sem("stacks_in0"), sem("stacks_in1")], sem("stored")
        dve_step = sem("dve_step")
        out_step = [sem("out_step0"), sem("out_step1")]
        act_step = sem("act_step")
        table_in = sem("table_in")
        pool_step = sem("pool_step")
        filled = sem("filled")
        rt_ask, rt_done = sem("rt_ask"), sem("rt_done")
        norm_ready, turned, turned_read, h_kept = map(sem, ("norm_ready", "turned", "turned_read", "h_kept"))
        qk_done, qk_squared, sums_done, roots_done, qn_done, qn_turned, qkh_done, qkl_done = map(sem, (
            "qk_done", "qk_squared", "sums_done", "roots_done", "qn_done", "qn_turned", "qkh_done", "qkl_done"))
        g_scored, g_exp, g_masked, g_prop, x1_done = map(sem, (
            "g_scored", "g_exp", "g_masked", "g_prop", "x1_done"))
        stats_done, u_done = sem("stats_done"), sem("u_done")
        proj_done, vh_done, v_done, rope_parts, rope_sum, qh_done, ql_done = map(sem, (
            "proj_done", "vh_done", "v_done", "rope_parts", "rope_sum", "qh_done", "ql_done"))
        a_ready, m_ready, negm_done = map(sem, ("a_ready", "m_ready", "negm_done"))
        a_free = [sem("a_free0"), sem("a_free1")]
        z_ready, out_taken = sem("z_ready"), sem("out_taken")
        e_full, eh_used = sem("e_full"), sem("eh_used")
        s_ready, e_ready, el_pool, el_dve, pv_done, ot_ready = map(sem, (
            "s_ready", "e_ready", "el_pool", "el_dve", "pv_done", "ot_ready"))
        w_halved = sem("w_halved")
        fh_done, fl_done, lg_done, lg_kept = map(sem, ("fh_done", "fl_done", "lg_done", "lg_kept"))
        gate_ready = sem("gate_ready")
        hid_done, silu_done, gated, gated_high, gated_low, y_done, acc_done = map(sem, (
            "hid_done", "silu_done", "gated", "gated_high", "gated_low", "y_done", "acc_done"))

        STACKS = 3 * NH + 3 * NKV
        STACKED = [(0, 4), (4, NB)]
        X_PARTS = [(0, 6), (6, 13), (13, 20), (20, NT)]
        STORED = [(0, 7), (7, 11), (11, NB)]
        block = ctx.enter_context(nc.Block())
        P2N, P4N = NB, 2 * NB
        UN = 2 * NB
        RING = 2

        def rows(v, n):
            return v.unsqueeze(2).to_broadcast([P, v.shape[1], n])

        def nat(i):
            return ps[:, bass.ds(1 + i % 2, 1), :].rearrange("p a c -> p (a c)")

        def qk_banks(i, k):
            return ps[:, bass.ds(1 + i % 2 * 2 + k, 1), :].rearrange("p a c -> p (a c)")

        def v_bank(i):
            return ps[:, bass.ds(5 + i % 2, 1), 0:2 * NKV * HD].rearrange("p a (t g d) -> p (a t) g d", t=2, g=NKV)

        def hidden(u):
            return ps[:, 3 * u:3 * u + 3, :].rearrange("p a c -> p (a c)")

        @block.sync
        def _(sp):
            for k, (t0, t1) in enumerate(X_PARTS):
                sp.dma_start(X1[:, t0:t1, :], x[:, t0:t1, :]).then_inc(x_in[k], 16)
            sp.dma_start(tab[:, :], tables).then_inc(tab_in, 16)
            sp.dma_start(small[:, :], w_small).then_inc(small_in, 16)
            sp.dma_start(tab16[:, :], tables16).then_inc(tab_in, 16)
            hj = NT // 2

            def load_adj(i, slot):
                for k in range(2):
                    sp.dma_start(adj2[:, slot, k * hj:(k + 1) * hj, :],
                                 adj[i, :, k * hj:(k + 1) * hj, :]).then_inc(adj_in[k], 16)
            load_adj(0, 0)
            for k in range(2):
                sp.wait_ge(adj_in[k], 16)
            load_adj(1, 1)
            for i in range(2, NB):
                sp.wait_ge(g_masked, RING + NT * (i - 1))
                for k in range(2):
                    sp.wait_ge(adj_in[k], 16 * i)
                load_adj(i, i % 2)
            sp.wait_ge(g_masked, RING + NT * (NB - 1))
            sp.dma_start(rope_f, rope).then_inc(rope_in, 16)
            for part, (b0, b1) in enumerate(STACKED):
                sp.wait_ge(ql_done, b1)
                sp.wait_ge(qh_done, b1)
                for h in range(NH):
                    for row, half in ((1, QKh), (2, QKh), (3, QKl)):
                        sp.dma_start(Qs[32 * row:32 * row + 32, b0:b1, h, :],
                                     half[HD * h:HD * h + HD, 0, b0 * BT:b1 * BT]
                                     .rearrange("p (b t) -> p b t", t=BT)).then_inc(stacks_in[part], 16)
                for g in range(NKV):
                    for row, half in ((1, QKh), (2, QKl), (3, QKh)):
                        sp.dma_start(Ks[32 * row:32 * row + 32, g, b0 * BT:b1 * BT],
                                     half[HD * g:HD * g + HD, 1, b0 * BT:b1 * BT]).then_inc(stacks_in[part], 16)
            for part in range(len(STACKED)):
                sp.wait_ge(stacks_in[part], 16 * STACKS)
            sp.dma_start(W1f, w1).then_inc(w_in, 16)
            sp.dma_start(W3f, w3).then_inc(w_in, 16)
            sp.wait_ge(w_halved, 2 * NE)
            sp.dma_start(W2f, w2).then_inc(w2_in, 16)
            for n, (b0, b1) in enumerate(STORED):
                sp.wait_ge(acc_done, (NE - 2) * NB + 2 * b1)
                sp.dma_start(out[:, 2 * b0:2 * b1, :], U[:, 2 * b0:2 * b1, :]).then_inc(stored, 16)
            sp.wait_ge(stored, 16 * len(STORED))

        @block.gpsimd
        def _(pool):
            pool.memset(H1[:, :, C:C + 1], 1.0).then_inc(filled, 1)
            pool.memset(zero16[:, :], 0.0).then_inc(filled, 1)
            pool.memset(bias[:, 0:1], LN_EPS).then_inc(filled, 1)
            pool.memset(bias[:, 1:2], RMS_EPS).then_inc(filled, 1)
            pool.memset(V16[:, :, :, HD:HD + 1], 1.0).then_inc(filled, 1)

            def keep_h(i):
                pool.wait_ge(norm_ready, i + 1)
                pool.tensor_tensor(H1[:, bass.ts(i, 2), 0:C], nb_[:, :, :],
                                   ones.unsqueeze(1).to_broadcast([P, 2, C]), ALU.mult).then_inc(h_kept, 1)
            pool.wait_ge(tab_in, 32)
            with pool.Fori(0, NB) as i:
                keep_h(i)

            pool.memset(Ks[0:32, :, :], 0.0).then_inc(pool_step, 1)
            pool.wait_ge(pool_step, 1)
            pool.memset(Ks[0:NH, :, :], 1.0).then_inc(filled, 1)

            pool.memset(Qs[0:32, :, :, :], 0.0).then_inc(filled, 1)

            def rope_add(i):
                pool.wait_ge(rope_parts, i + 1)
                wait(pool, qh_done, i)
                pool.tensor_tensor(qr, ra, rb, ALU.add).then_inc(rope_sum, 1)

            def q_low(i):
                pool.wait_ge(qh_done, i + 1)
                pool.tensor_tensor(QKl[:, :, bass.ts(i, BT)], qr.rearrange("p (a t) -> p a t", a=2),
                                   QKh[:, :, bass.ts(i, BT)], ALU.subtract).then_inc(ql_done, 1)
                pool.wait_ge(ql_done, i + 1)
            skewed(pool, NB, [(1, q_low), (0, rope_add)])

            n = Count(pool, "tiles", 1)
            n_e = Count(pool, "tiles_e", 1 + RING)

            def e_low_pair(*columns):
                for u in range(2):
                    pc = columns[u]
                    pool.wait_ge(e_ready, n_e.now())
                    pool.wait_ge(pv_done, n.now())
                    pool.tensor_tensor(EL[u][:, 0:pc], E[u][:, 0:pc], EH[u][:, 0:pc],
                                       ALU.subtract).then_inc(el_pool, 1)
                    n.up()
                    n_e.up()

            pool.sem_inc(el_pool, RING)
            e_low_pair(1024, 1024)
            e_low_pair(1024, 1024)
            e_low_pair(1024, PC)
            with pool.Fori(2, NB - 2) as i:
                e_low_pair(1024, 1024)
                e_low_pair(1024, PC)
                with pool.Fori(1, i):
                    e_low_pair(PC, PC)
            for i in (NB - 2, NB - 1):
                with pool.Fori(0, i + 1):
                    e_low_pair(PC, PC)

            pool.wait_ge(norm_ready, P4N + NB)
            pool.tensor_tensor(U[:, :, :], U[:, :, :], X1[:, :, :], ALU.add).then_inc(u_done, 1)

            def gated_rest(m, u):
                pool.wait_ge(gated_high, m + 1)
                wait(pool, y_done, m - 1)
                pool.tensor_tensor(hhl[u], hh_[u], hhh[u], ALU.subtract).then_inc(gated_low, 1)
            for u in range(2):
                gated_rest(u, u)
            with pool.Fori(1, NE // 2 * NB) as k:
                for u in range(2):
                    gated_rest(k * 2 + u, u)

        @block.scalar
        def _(act):
            def roots(n, eps):
                act.wait_ge(rt_ask, n)
                act.activation(stat[:, 2, :], stat[:, 1, :], ACT.Sqrt, bias=bias[:, eps:eps + 1]).then_inc(rt_done, 1)

            act.wait_ge(filled, 5)
            roots(1, 0)

            def turned_copy(i):
                act.wait_ge(turned, i + 1)
                wait(act, qk_done, i)
                act.activation(tb[:, :], ps[:, 0, 0:BT], ACT.Copy).then_inc(turned_read, 1)

            def qk_square(i):
                act.wait_ge(qk_done, i + 1)
                wait(act, sums_done, i)
                act.activation(sq, nat(i), ACT.Square).then_inc(qk_squared, 1)

            def qk_root(i):
                act.wait_ge(sums_done, i + 1)
                wait(act, qn_done, i)
                act.activation(ss4[:, 1, :], ss4[:, 0, :], ACT.Sqrt).then_inc(roots_done, 1)

            def qk_high(i):
                act.wait_ge(qn_turned, i + 1)
                act.activation(QKh[:, :, bass.ts(i, BT)], ps[:, 3, :].rearrange("p (a t) -> p a t", a=2),
                               ACT.Copy).then_inc(qkh_done, 1)
            skewed(act, NB, [(4, qk_high), (3, qk_root), (0, turned_copy), (1, qk_square)])

            def g_exps(m, u):
                act.wait_ge(g_scored, m + 1)
                act.wait_ge(g_masked, m + 1)
                act.activation(Eg[u], ps[:, u, 0:BT], ACT.Exp, scale=1.0 / (UNIT * UNIT)).then_inc(g_exp, 1)

            tables_loaded = 0

            def load_table(func):
                nonlocal tables_loaded
                act.activation(unused[:, tables_loaded:tables_loaded + 1], bias[:, 0:1], func).then_inc(table_in, 1)
                tables_loaded += 1
            load_table(ACT.Exp)
            act.sem_inc(g_exp, RING)
            with act.Fori(0, NB * NB) as k:
                for u in range(2):
                    g_exps(k * 2 + u, u)

            roots(2, 0)
            roots(3, 1)

            def q_turned(i):
                act.wait_ge(turned, P2N + i + 1)
                wait(act, proj_done, i)
                act.activation(tb[:, :], ps[:, 0, 0:BT], ACT.Copy, scale=ln1).then_inc(turned_read, 1)

            def v_high(i):
                act.wait_ge(proj_done, i + 1)
                act.activation(V16[:, bass.ts(i, 2), :, 0:HD], v_bank(i), ACT.Copy).then_inc(vh_done, 1)

            def q_high(i):
                act.wait_ge(rope_sum, i + 1)
                act.activation(QKh[:, :, bass.ts(i, BT)], qr.rearrange("p (a t) -> p a t", a=2),
                               ACT.Copy).then_inc(qh_done, 1)
            skewed(act, NB, [(3, q_high), (0, q_turned), (1, v_high)])

            load_table(ACT.Exp)
            n = Count(act, "act_tiles", 1)
            done = Count(act, "act_used", 0)

            z_turn = Count(act, "z_turn", 1)
            z_slot = Count(act, "z_slot", 1)

            def exp_tile(u):
                pair_of_banks = ps[:, 2 + 2 * u:4 + 2 * u, :].rearrange("p a c -> p (a c)")
                act.wait_ge(s_ready, n.now())
                act.wait_ge(el_pool, n.now())
                act.wait_ge(el_dve, n.now())
                act.activation(E[u], pair_of_banks, ACT.Exp, scale=SCALE).then_inc(e_full, 1)
                act.wait_ge(eh_used, n.now())
                act.activation(EH[u], pair_of_banks, ACT.Exp, scale=SCALE).then_inc(e_ready, 1)
                n.up()
                done.up()

            def exp_pair():
                for u in range(2):
                    exp_tile(u)

            def keep_output(g):
                if g == 0:
                    act.wait_ge(out_taken, z_slot.now())
                    z_slot.up()
                for t in range(2):
                    act.wait_ge(z_ready, z_turn.now())
                    act.activation(Z[:, g, t, :], ps[:, t, 0:2 * (C + 1)], ACT.Copy).then_inc(a_free[t], 1)
                    z_turn.up()

            def out_copy():
                act.wait_ge(pv_done, done.now())
                act.activation(OT[0:VW, :, :], ps[0:VW, 6:8, :], ACT.Copy).then_inc(ot_ready, 1)

            def attention_exps(i):
                exp_pair()
                out_copy()
                for u in range(2):
                    exp_tile(u)
                    keep_output(u)

            act.sem_inc(e_ready, RING)
            act.sem_inc(pv_done, RING)
            act.sem_inc(eh_used, RING)
            exp_pair()
            attention_exps(1)
            with act.Fori(2, NB - 1) as i:
                attention_exps(i)
                with act.Fori(1, i):
                    exp_pair()
            attention_exps(NB - 1)
            exp_pair()
            roots(4, 1)
            load_table(ACT.Exp)
            with act.Fori(2, NB - 1):
                exp_pair()
            done.up(2)
            out_copy()
            for g in range(NKV):
                keep_output(g)

            load_table(ACT.Sqrt)
            roots(5, 1)

            def silu(m, u):
                act.wait_ge(hid_done, m + 1)
                act.wait_ge(gated, m + 1)
                act.activation(sl[u], hidden(u)[:, 0:HC * BT], ACT.Silu).then_inc(silu_done, 1)

            def gated_highs(m, u):
                act.wait_ge(gated, m + 1 + RING)
                wait(act, y_done, m - 1)
                act.activation(hhh[u], hh_[u], ACT.Copy).then_inc(gated_high, 1)
            load_table(ACT.Silu)
            for u in range(2):
                silu(u, u)
                gated_highs(u, u)
            act.wait_ge(gate_ready, 1)
            act.activation(R[1][:, :, :], R[0][:, :, :], ACT.Exp).then_inc(act_step, 1)
            load_table(ACT.Silu)
            with act.Fori(1, NE // 2 * NB) as k:
                for u in range(2):
                    silu(k * 2 + u, u)
                    gated_highs(k * 2 + u, u)

        @block.vector
        def _(dve):
            own = Count(dve, "own", 0)

            def link(ins):
                ins.then_inc(dve_step, 1)
                own.up()
                dve.wait_ge(dve_step, own.now())

            def tile_of(v, i, t):
                return v[:, bass.ds(i * 2 + t, 1), :].rearrange("p a c -> p (a c)")

            def row_moments(mean, var):
                me, mo, ve, vo = (st6[:, :, k] for k in (1, 4, 2, 5))
                link(dve.tensor_tensor(mean, me, mo, ALU.add))
                link(dve.tensor_scalar(mean, mean, 0.5, None, ALU.mult))
                link(dve.tensor_tensor(stat[:, 6, :], me, mo, ALU.subtract))
                link(dve.scalar_tensor_tensor(out=stat[:, 6, :], in0=stat[:, 6, :], scalar=0.25,
                                              in1=stat[:, 6, :], op0=ALU.mult, op1=ALU.mult))
                link(dve.tensor_tensor(stat[:, 7, :], ve, vo, ALU.add))
                link(dve.scalar_tensor_tensor(out=var, in0=stat[:, 7, :], scalar=1.0 / C, in1=stat[:, 6, :],
                                              op0=ALU.mult, op1=ALU.add))

            def one_over_root(n, dst):
                dve.sem_inc(rt_ask, 1)
                dve.wait_ge(rt_done, n)
                link(dve.reciprocal(dst, stat[:, 2, :]))

            MEAN, VAR, RSTD, RBOTH = stat[:, 0, :], stat[:, 1, :], stat[:, 3, :], stat[:, 4, :]

            def layernormed(dst, i, t, scale):
                return dve.tensor_scalar(dst, tile_of(X1, i, t), MEAN[:, bass.ds(i * 2 + t, 1)],
                                         scale[:, bass.ds(i * 2 + t, 1)], ALU.subtract, ALU.mult)

            for k, (t0, t1) in enumerate(X_PARTS):
                dve.wait_ge(x_in[k], 16)
                for t in range(t0, t1):
                    dve.bn_stats(st6[:, t, :], X1[:, t, :]).then_inc(stats_done, 1)
            dve.wait_ge(stats_done, NT)
            row_moments(MEAN, VAR)
            one_over_root(1, RSTD)

            def normalized(i):
                wait(dve, turned, i)
                wait(dve, h_kept, i)
                for t in range(2):
                    ins = layernormed(nb_[:, t, :], i, t, RSTD)
                ins.then_inc(norm_ready, 1)

            def qk_sums(i):
                dve.wait_ge(qk_squared, i + 1)
                dve.tensor_reduce(ss4[:, 0, :], sq.rearrange("p (a c) -> p a c", a=4), X, ALU.add
                                  ).then_inc(sums_done, 1)

            def qk_norm(i):
                dve.wait_ge(roots_done, i + 1)
                wait(dve, qn_turned, i)
                link(dve.tensor_scalar(ss4[:, 1, :], ss4[:, 1, :], COS_EPS, 1.0 / UNIT, ALU.max, ALU.mult))
                link(dve.reciprocal(ss4[:, 1, :], ss4[:, 1, :]))
                dve.tensor_tensor(qn.rearrange("p (a c) -> p a c", a=4),
                                  nat(i).rearrange("p (a c) -> p a c", a=4),
                                  rows(ss4[:, 1, :], C), ALU.mult).then_inc(qn_done, 1)

            def qk_low(i):
                dve.wait_ge(qkh_done, i + 1)
                dve.tensor_tensor(QKl[:, :, bass.ts(i, BT)], ps[:, 3, :].rearrange("p (a t) -> p a t", a=2),
                                  QKh[:, :, bass.ts(i, BT)], ALU.subtract).then_inc(qkl_done, 1)
            skewed(dve, NB, [(0, normalized), (3, qk_norm), (2, qk_sums), (4, qk_low)])

            def mask(m, u, adj_tile):
                dve.wait_ge(g_exp, m + 1 + RING)
                wait(dve, g_prop, m - 1)
                dve.scalar_tensor_tensor(out=Em[u], in0=adj_tile, scalar=0.0, in1=Eg[u],
                                         op0=ALU.is_gt, op1=ALU.mult).then_inc(g_masked, 1)

            def adj_tile(slot, jt):
                return adj2[:, bass.ds(slot, 1), bass.ds(jt, 1), :].rearrange("p a b c -> p (a b c)")

            has, inv, keep = gs[:, 0:2], gs[:, 2:4], gs[:, 4:6]

            def g_result(i):
                return ps[:, bass.ds(4 + i % 2, 1), :].rearrange("p a c -> p (a c)")[:, 0:2 * (C + 1)] \
                    .rearrange("p (t c) -> p t c", t=2)

            def sums_of(i):
                return g_result(i)[:, :, C:C + 1].rearrange("p t c -> p (t c)")

            def shares_1(i):
                dve.wait_ge(g_prop, NT * (i + 1))
                link(dve.tensor_scalar(has, sums_of(i), 0.0, None, ALU.is_gt))
                link(dve.scalar_tensor_tensor(out=inv, in0=sums_of(i), scalar=1.0, in1=has, op0=ALU.add,
                                              op1=ALU.subtract))

            def shares_2(i):
                link(dve.reciprocal(inv, inv))
                link(dve.scalar_tensor_tensor(out=inv, in0=inv, scalar=0.5, in1=has, op0=ALU.mult, op1=ALU.mult))
                link(dve.tensor_scalar(keep, has, -0.5, 1.0, ALU.mult, ALU.add))

            def blend_1(i, t):
                link(dve.scalar_tensor_tensor(out=gt[:, t, :], in0=g_result(i)[:, t, 0:C], scalar=inv[:, t:t + 1],
                                              in1=tile_of(X1, i, t), op0=ALU.mult, op1=ALU.add))

            def blend_2(i, t):
                dve.scalar_tensor_tensor(
                    out=tile_of(X1, i, t), in0=H1[:, bass.ds(i * 2 + t, 1), 0:C].rearrange("p a c -> p (a c)"),
                    scalar=keep[:, t:t + 1], in1=gt[:, t, :], op0=ALU.mult, op1=ALU.add).then_inc(x1_done, 1)

            def x1_moments(i):
                dve.wait_ge(x1_done, (i + 1) * 2)
                for t in range(2):
                    dve.bn_stats(st6[:, bass.ds(i * 2 + t, 1), :].rearrange("p a c -> p (a c)"),
                                 tile_of(X1, i, t)).then_inc(stats_done, 1)

            dve.sem_inc(g_masked, RING)
            for k in range(2):
                dve.wait_ge(adj_in[k], 16)
            for u in range(2):
                mask(u, u, adj_tile(0, u))
            with dve.Fori(1, NB) as j:
                for u in range(2):
                    mask(j * 2 + u, u, adj_tile(0, j * 2 + u))
            with dve.Fori(1, NB) as i:
                slot = dve.snap(i % 2)
                for k in range(2):
                    dve.wait_ge(adj_in[k], 16 * (i + 1))
                m0 = i * NT
                mask(m0, 0, adj_tile(slot, 0))
                mask(m0 + 1, 1, adj_tile(slot, 1))
                shares_1(i - 1)
                mask(m0 + 2, 0, adj_tile(slot, 2))
                shares_2(i - 1)
                mask(m0 + 3, 1, adj_tile(slot, 3))
                blend_1(i - 1, 0)
                mask(m0 + 4, 0, adj_tile(slot, 4))
                blend_2(i - 1, 0)
                blend_1(i - 1, 1)
                mask(m0 + 5, 1, adj_tile(slot, 5))
                blend_2(i - 1, 1)
                mask(m0 + 6, 0, adj_tile(slot, 6))
                x1_moments(i - 1)
                mask(m0 + 7, 1, adj_tile(slot, 7))
                with dve.Fori(4, NB) as j:
                    for u in range(2):
                        mask(m0 + j * 2 + u, u, adj_tile(slot, j * 2 + u))
            shares_1(NB - 1)
            shares_2(NB - 1)
            for t in range(2):
                blend_1(NB - 1, t)
                blend_2(NB - 1, t)
            x1_moments(NB - 1)

            dve.wait_ge(stats_done, 2 * NT)
            row_moments(MEAN, VAR)
            one_over_root(2, RSTD)
            link(dve.tensor_tensor(VAR, VAR, RSTD, ALU.mult))
            link(dve.tensor_tensor(VAR, VAR, RSTD, ALU.mult))
            one_over_root(3, RBOTH)
            link(dve.tensor_tensor(RBOTH, RBOTH, RSTD, ALU.mult))

            def both_normalized(i):
                wait(dve, turned, P2N + i)
                for t in range(2):
                    ins = layernormed(nb_[:, t, :], i, t, RBOTH)
                ins.then_inc(norm_ready, 1)
                for t in range(2):
                    layernormed(tile_of(U, i, t), i, t, RSTD).then_inc(u_done, 1)

            def rope_halves(i):
                dve.wait_ge(proj_done, i + 1)
                wait(dve, rope_sum, i)
                for k, dst in ((0, ra), (1, rb)):
                    ins = dve.tensor_tensor(dst.rearrange("p (a t) -> p a t", a=2),
                                            qk_banks(i, k).rearrange("p (a t) -> p a t", a=2),
                                            rope_f[:, k, bass.ts(i, BT)].unsqueeze(1).to_broadcast([P, 2, BT]),
                                            ALU.mult)
                ins.then_inc(rope_parts, 1)

            def v_low(i):
                dve.wait_ge(vh_done, i + 1)
                dve.tensor_tensor(V16[:, bass.ts(i, 2), :, HD + 1:VW], v_bank(i),
                                  V16[:, bass.ts(i, 2), :, 0:HD], ALU.subtract).then_inc(v_done, 1)
            dve.wait_ge(rope_in, 16)
            skewed(dve, NB, [(0, both_normalized), (2, rope_halves), (2, v_low)])

            a = Count(dve, "a", 1)
            a_freed = [Count(dve, f"a_freed{u}", 1) for u in range(2)]
            n = Count(dve, "tiles", 1)
            n_e = Count(dve, "tiles_e", 1 + RING)

            def a_bank(s):
                return ps[:, s, :]

            def chunk_max(j, t, diagonal=False):
                keys = P if diagonal and t == 0 else BT
                for g in range(NKV):
                    dve.wait_ge(a_ready, a.now())
                    dve.tensor_reduce(cm[:, t, 2 * g:2 * g + 2, bass.ds(j, 1)].rearrange("p h j -> p (h j)"),
                                      a_bank(g).rearrange("p (h k) -> p h k", h=2)[:, :, 0:keys], X, ALU.max
                                      ).then_inc(a_free[g], 1)
                    a.up()
                    a_freed[g].up()

            def block_max():
                for u in range(2):
                    dve.wait_ge(a_free[u], a_freed[u].now())
                link(dve.tensor_reduce(m8[:, :, :].rearrange("p t h -> p (t h)"),
                                       cm[:, :, :, :].rearrange("p t h j -> p (t h) j"), X, ALU.max))
                dve.sem_inc(m_ready, 1)

            def negated_max(i):
                for t in range(2):
                    dve.wait_ge(a_ready, a.now())
                    dve.tensor_tensor(Qs[0:NH, bass.ds(i, 1), :, t * P:t * P + P].rearrange("p a h t -> p (a h) t"),
                                      a_bank(t)[0:NH, 0:P].unsqueeze(1).to_broadcast([NH, NH, P]),
                                      negblk, ALU.mult).then_inc(a_free[t], 1)
                    a.up()
                    a_freed[t].up()
                for u in range(2):
                    dve.wait_ge(a_free[u], a_freed[u].now())
                dve.sem_inc(negm_done, 1)

            def e_low(u, all_of_pool=False):
                if all_of_pool:
                    dve.sem_inc(el_dve, 1)
                else:
                    dve.wait_ge(e_ready, n_e.now())
                    dve.wait_ge(pv_done, n.now())
                    dve.tensor_tensor(EL[u][:, PC:1024], E[u][:, PC:1024], EH[u][:, PC:1024],
                                      ALU.subtract).then_inc(el_dve, 1)
                n.up()
                n_e.up()

            out_own = [Count(dve, f"out_own{t}", 0) for t in range(2)]

            def attention_out(i, g):
                def step(t, ins):
                    ins.then_inc(out_step[t], 1)
                    out_own[t].up()
                z = [Z[:, g, t, :].rearrange("p (h c) -> p h c", h=2) for t in range(2)]
                for t in range(2):
                    a_freed[t].up()
                    dve.wait_ge(a_free[t], a_freed[t].now())
                    step(t, dve.reciprocal(zr[:, 2 * t:2 * t + 2], z[t][:, :, C:C + 1].rearrange("p h c -> p (h c)")))
                for h in range(2):
                    for t in range(2):
                        dve.wait_ge(out_step[t], out_own[t].now())
                        ins = dve.scalar_tensor_tensor(out=tile_of(U, i, t), in0=z[t][:, h, 0:C],
                                                       scalar=zr[:, 2 * t + h:2 * t + h + 1], in1=tile_of(U, i, t),
                                                       op0=ALU.mult, op1=ALU.add)
                        step(t, ins)
                for t in range(2):
                    dve.wait_ge(out_step[t], out_own[t].now())
                    if g == NKV - 1:
                        dve.bn_stats(st6[:, bass.ds(i * 2 + t, 1), :].rearrange("p a c -> p (a c)"),
                                     tile_of(U, i, t)).then_inc(stats_done, 1)
                if g == NKV - 1:
                    dve.sem_inc(out_taken, 1)

            for u in range(2):
                dve.sem_inc(a_free[u], 1)
            dve.sem_inc(out_taken, 1)
            dve.sem_inc(el_dve, RING)
            dve.sem_inc(gated, RING)
            link(dve.memset(cm[:, :, :, :], LOWEST))
            for t in range(2):
                chunk_max(0, t, diagonal=True)
            block_max()
            negated_max(0)
            for j in (1, 0):
                for t in range(2):
                    chunk_max(j, t, diagonal=j == 1)
            block_max()

            def attention_steps(j, after=False):
                for t in range(2):
                    if after:
                        chunk_max(j, t)
                    e_low(1 - t)

            def attention_block(i, after=True, negate=True, inner=None):
                if after:
                    chunk_max(i + 2, 0, diagonal=True)
                    chunk_max(i + 2, 1)
                e_low(0, after)
                if negate:
                    negated_max(i + 1)
                if after:
                    chunk_max(i + 1, 0)
                e_low(1, after)
                if after:
                    chunk_max(i + 1, 1)
                e_low(0, after)
                attention_out(i - 1, 0)
                attention_out(i - 1, 1)
                if inner:
                    inner()
                elif not (isinstance(i, int) and i == 1):
                    with dve.Fori(1, i) as j:
                        attention_steps(j, after)
                if after:
                    chunk_max(i, 0)
                    chunk_max(i, 1)
                e_low(1)
                if after:
                    chunk_max(0, 0)
                    chunk_max(0, 1)
                    block_max()

            chunk_max(2, 0, diagonal=True)
            chunk_max(2, 1)
            negated_max(1)
            e_low(0, True)
            chunk_max(1, 0)
            chunk_max(1, 1)
            e_low(1, True)
            chunk_max(0, 0)
            chunk_max(0, 1)
            block_max()
            attention_block(1)
            with dve.Fori(2, NB - 2) as i:
                attention_block(i)
            def in_halves(e, weights):
                for full, high, low in weights:
                    link(dve.tensor_copy(high[:, bass.ts(e, HW)], full[:, bass.ts(e, HW)]))
                    dve.tensor_tensor(low[:, bass.ts(e, HW)], full[:, bass.ts(e, HW)], high[:, bass.ts(e, HW)],
                                      ALU.subtract).then_inc(w_halved, 1)

            def weights_along():
                dve.wait_ge(w_in, 32)
                with dve.Fori(1, NE + 1) as j:
                    attention_steps(j)
                    in_halves(j - 1, ((W1f, W1h, W1l), (W3f, W3h, W3l)))
                with dve.Fori(NE + 1, NB - 2) as j:
                    attention_steps(j)

            def mean_squares():
                row_moments(MEAN, VAR)
                link(dve.tensor_tensor(MEAN, MEAN, MEAN, ALU.mult))
                link(dve.tensor_tensor(VAR, VAR, MEAN, ALU.add))

            def rms_normalized(i):
                wait(dve, turned, P4N + i)
                dve.tensor_tensor(nb_[:, :, :], U[:, bass.ts(i, 2), :],
                                  rows(RSTD[:, bass.ts(i, 2)], C), ALU.mult).then_inc(norm_ready, 1)

            def f_halves(i):
                dve.wait_ge(turned, P4N + i + 1)
                wait(dve, lg_done, i)
                link(dve.tensor_scalar(tb[:, :], ps[:, 0, 0:BT], ln2, None, ALU.mult))
                dve.sem_inc(turned_read, 1)
                dve.tensor_copy(F16h[:, bass.ts(i, BT)], tb[:, :]).then_inc(fh_done, 1)
                dve.wait_ge(fh_done, i + 1)
                dve.tensor_tensor(F16l[:, bass.ts(i, BT)], tb[:, :], F16h[:, bass.ts(i, BT)],
                                  ALU.subtract).then_inc(fl_done, 1)

            def keep_logits(i):
                dve.wait_ge(lg_done, i + 1)
                dve.tensor_copy(LG[:, bass.ts(i, 2), :], ps[:, 1, 0:2 * NE].rearrange("p (t e) -> p t e", t=2)
                                ).then_inc(lg_kept, 1)

            def normalized_along(j, e=None):
                b = j - 2
                if not isinstance(b, int):
                    keep_logits(b - 1)
                e_low(1)
                f_halves(b)
                e_low(0)
                rms_normalized(b + 1)
                if e is not None:
                    in_halves(e, ((W2f, W2h, W2l),))

            def w2_and_rows_along():
                dve.wait_ge(stats_done, 3 * NT - 2)
                mean_squares()
                dve.sem_inc(rt_ask, 1)
                dve.wait_ge(w2_in, 16)
                attention_steps(1)
                in_halves(0, ((W2f, W2h, W2l),))
                dve.wait_ge(rt_done, 4)
                link(dve.reciprocal(RSTD, stat[:, 2, :]))
                rms_normalized(0)
                normalized_along(2, 1)
                with dve.Fori(3, NE + 1) as j:
                    normalized_along(j, j - 1)
                with dve.Fori(NE + 1, NB - 1) as j:
                    normalized_along(j)

            attention_block(NB - 2, after=False, inner=weights_along)
            attention_block(NB - 1, after=False, negate=False, inner=w2_and_rows_along)
            keep_logits(NB - 4)
            f_halves(NB - 3)
            rms_normalized(NB - 2)
            keep_logits(NB - 3)
            f_halves(NB - 2)
            keep_logits(NB - 2)
            for g in range(NKV):
                attention_out(NB - 1, g)
            dve.wait_ge(stats_done, 3 * NT)
            mean_squares()
            one_over_root(5, RSTD)
            rms_normalized(NB - 1)
            f_halves(NB - 1)
            keep_logits(NB - 1)

            def gate(m, u):
                dve.wait_ge(silu_done, m + 1)
                wait(dve, gated_low, m - 1)
                dve.tensor_tensor(hh_[u], hidden(u)[:, HC * BT:2 * HC * BT], sl[u], ALU.mult).then_inc(gated, 1)

            dve.wait_ge(lg_kept, NB)
            big, tot, r = rs[:, 0, :], rs[:, 1, :], R
            revb = rev.unsqueeze(1).to_broadcast([P, NT, NE])
            link(dve.tensor_reduce(big, LG[:, :, :], X, ALU.max))
            dve.tensor_tensor(r[0][:, :, :], LG[:, :, :], rows(big, NE), ALU.subtract).then_inc(gate_ready, 1)
            gate(0, 0)
            gate(1, 1)
            dve.wait_ge(act_step, 1)
            link(dve.tensor_reduce(tot, r[1][:, :, :], X, ALU.add))
            link(dve.reciprocal(tot, tot))
            link(dve.tensor_tensor(r[1][:, :, :], r[1][:, :, :], rows(tot, NE), ALU.mult))

            def first_largest(probs, dst, top, pick):
                link(dve.tensor_reduce(top, probs, X, ALU.max))
                link(dve.tensor_tensor(dst, probs, rows(top, NE), ALU.is_equal))
                link(dve.tensor_tensor(dst, dst, revb, ALU.mult))
                link(dve.tensor_reduce(pick, dst, X, ALU.max))
                link(dve.tensor_tensor(dst, dst, rows(pick, NE), ALU.is_equal))
            first_largest(r[1][:, :, :], r[0][:, :, :], rs[:, 2, :], rs[:, 3, :])
            link(dve.scalar_tensor_tensor(out=r[2][:, :, :].rearrange("p t e -> p (t e)"),
                                          in0=r[0][:, :, :].rearrange("p t e -> p (t e)"), scalar=-2.0,
                                          in1=r[1][:, :, :].rearrange("p t e -> p (t e)"),
                                          op0=ALU.mult, op1=ALU.add))
            first_largest(r[2][:, :, :], r[3][:, :, :], rs[:, 4, :], rs[:, 5, :])
            link(dve.tensor_tensor(r[0][:, :, :], r[0][:, :, :], r[3][:, :, :], ALU.add))
            link(dve.scalar_tensor_tensor(out=tot, in0=rs[:, 2, :], scalar=1e-9, in1=rs[:, 4, :],
                                          op0=ALU.add, op1=ALU.add))
            link(dve.reciprocal(tot, tot))
            link(dve.tensor_tensor(r[0][:, :, :], r[0][:, :, :], r[1][:, :, :], ALU.mult))
            link(dve.tensor_tensor(GW[:, :, :], r[0][:, :, :], rows(tot, NE), ALU.mult))
            dve.wait_ge(u_done, UN + 1)

            def add_expert(m, e, i, u):
                dve.wait_ge(y_done, m + 1)
                wait(dve, acc_done, m)
                for t in range(2):
                    ut = U[:, bass.ds(i * 2 + t, 1), :].rearrange("p a c -> p (a c)")
                    ins = dve.scalar_tensor_tensor(
                        out=ut, in0=ps[:, 6 + u, t * C:(t + 1) * C],
                        scalar=GW[:, bass.ds(i * 2 + t, 1), bass.ds(e, 1)].rearrange("p a c -> p (a c)"),
                        in1=ut, op0=ALU.mult, op1=ALU.add)
                ins.then_inc(acc_done, 1)

            def expert_turn(e2, i, nxt):
                m = e2 * (2 * NB) + i * 2
                for u in range(2):
                    if nxt:
                        gate(m + 2 + u, u)
                    add_expert(m + u, e2 * 2 + u, i, u)

            expert_turn(0, 0, True)
            with dve.Fori(1, NB) as i:
                expert_turn(0, i, True)
            with dve.Fori(1, NE // 2 - 1) as e2:
                with dve.Fori(0, NB) as i:
                    expert_turn(e2, i, True)
            with dve.Fori(0, NB - 1) as i:
                expert_turn(NE // 2 - 1, i, True)
            expert_turn(NE // 2 - 1, NB - 1, False)

        @block.tensor
        def _(pe):
            def turn(n):
                pe.wait_ge(norm_ready, n + 1)
                wait(pe, turned_read, n)
                for t in range(2):
                    ins = pe.transpose(ps[:, 0, t * P:(t + 1) * P], nb_[:, t, :], ident)
                ins.then_inc(turned, 1)

            pe.wait_ge(tab_in, 32)
            pe.wait_ge(small_in, 16)
            pe.wait_ge(filled, 5)

            def qk(i):
                pe.wait_ge(turned_read, i + 1)
                wait(pe, qn_done, i - 1)
                for t in range(2):
                    ins = pe.matmul(nat(i)[:, t * 2 * C:(t + 1) * 2 * C], tb[:, t * P:(t + 1) * P], Wqk,
                                    start=True, stop=True)
                ins.then_inc(qk_done, 1)

            def qk_turn(i):
                pe.wait_ge(qn_done, i + 1)
                wait(pe, qkl_done, i)
                for t in range(2):
                    for k in range(2):
                        ins = pe.transpose(ps[:, 3, k * BT + t * P:k * BT + (t + 1) * P],
                                           qn[:, (2 * t + k) * C:(2 * t + k + 1) * C], ident)
                ins.then_inc(qn_turned, 1)
            skewed(pe, NB, [(4, qk_turn), (0, turn), (1, qk)])

            def g_scores(i, jt, u, m):
                pe.wait_ge(g_exp, m + 1)
                parts = ((QKh, QKh), (QKh, QKl), (QKl, QKh))
                for k, (qa, ka) in enumerate(parts):
                    ins = pe.matmul(ps[:, u, 0:BT], qa[:, 0, bass.ts(jt, P)], ka[:, 1, bass.ts(i, BT)],
                                    start=(k == 0), stop=(k == len(parts) - 1))
                ins.then_inc(g_scored, 1)

            def g_bank(slot):
                return ps[:, bass.ds(4 + slot, 1), :].rearrange("p a c -> p (a c)")

            def g_clear(i, slot):
                wait(pe, x1_done, (i - 1) * 2)
                pe.matmul(g_bank(slot)[:, 0:2 * (C + 1)], zero16[:, 0:P], zero16[:, 0:2 * (C + 1)],
                          start=True, stop=False, skip_group_check=True)

            def g_propagate(slot, jt, u, m):
                pe.wait_ge(g_masked, m + 1 + RING)
                for t in range(2):
                    ins = pe.matmul(g_bank(slot)[:, t * (C + 1):(t + 1) * (C + 1)], Em[u][:, t * P:(t + 1) * P],
                                    H1[:, bass.ds(jt, 1), :].rearrange("p a c -> p (a c)"),
                                    start=False, stop=False, skip_group_check=True)
                ins.then_inc(g_prop, 1)

            def g_block(i, nxt):
                slot = i % 2 if isinstance(i, int) else pe.snap(i % 2)
                g_clear(i, slot)
                with pe.Fori(0, NB - 1) as j:
                    for u in range(2):
                        m = i * NT + j * 2 + u
                        g_scores(i, j * 2 + 2 + u, u, m + 2)
                        g_propagate(slot, j * 2 + u, u, m)
                for u in range(2):
                    m = i * NT + NT - 2 + u
                    if nxt:
                        g_scores(i + 1, u, u, m + 2)
                    g_propagate(slot, NT - 2 + u, u, m)

            pe.wait_ge(qkl_done, NB)
            pe.wait_ge(h_kept, NB)
            for u in range(2):
                g_scores(0, u, u, u)
            g_block(0, True)
            g_block(1, True)
            with pe.Fori(2, NB - 1) as i:
                g_block(i, True)
            g_block(NB - 1, False)

            def project(i):
                pe.wait_ge(turned_read, P2N + i + 1)
                wait(pe, rope_parts, i - 1)
                wait(pe, v_done, i - 1)
                for k in range(4):
                    pe.matmul(qk_banks(i, k // 2)[:, (k % 2) * BT:(k % 2 + 1) * BT], Wf[:, k * P:(k + 1) * P], tb[:, :],
                              start=True, stop=True)
                for t in range(2):
                    ins = pe.matmul(v_bank(i)[:, t, :, :].rearrange("p g d -> p (g d)"), tb[:, t * P:(t + 1) * P], Wv,
                                    start=True, stop=True)
                ins.then_inc(proj_done, 1)
            skewed(pe, NB, [(0, lambda i: turn(P2N + i)), (1, project)])

            pe.wait_ge(stacks_in[0], 16 * STACKS)
            pe.wait_ge(filled, 7)
            pe.wait_ge(rope_parts, NB)
            pe.wait_ge(v_done, NB)
            a = [Count(pe, f"a_slot{u}", 1) for u in range(2)]
            s = Count(pe, "s_slot", 1)
            v = Count(pe, "v_tile", 1 + RING)

            def a_task(u, fill, ready=a_ready):
                pe.wait_ge(a_free[u], a[u].now())
                fill(ps[:, u, :]).then_inc(ready, 1)
                a[u].up()

            def row_part(i, j, t, g, diagonal=False):
                def fill(bank):
                    if diagonal:
                        pe.matmul(bank, ident16, maskA[:, t, :], start=True, stop=False,
                                  skip_group_check=True)
                    for h in range(2):
                        ins = pe.matmul(bank[:, h * BT:(h + 1) * BT],
                                        Qs[:, bass.ds(i, 1), 2 * g + h, t * P:(t + 1) * P]
                                        .rearrange("p a t -> p (a t)"),
                                        Ks[:, g, bass.ts(j, BT)], start=not diagonal, stop=True,
                                        skip_group_check=True)
                    return ins
                a_task(g, fill)

            def row_chunk(i, j, t, diagonal=False):
                for g in range(NKV):
                    row_part(i, j, t, g, diagonal)

            def maxima(i):
                pe.wait_ge(m_ready, i + 1)
                for t in range(2):
                    a_task(t, lambda bank: pe.transpose(bank[0:NH, 0:P], m8[:, t, :], ident))

            def scores(i, j, u, diagonal=False):
                pe.wait_ge(e_ready, s.now())
                for g in range(NKV):
                    bank = ps[:, 2 + 2 * u + g, :]
                    ins = pe.matmul(bank, Ks[:, g, bass.ts(j * 2 + u, P)],
                                    Qs[:, bass.ds(i, 1), 2 * g:2 * g + 2, :].rearrange("p a h t -> p (a h t)"),
                                    start=True, stop=not diagonal)
                    if diagonal:
                        ins = pe.matmul(bank, ident16, maskB[:, u, :], start=False, stop=True)
                ins.then_inc(s_ready, 1)
                s.up()

            def values(j, u, first=False, rows=None):
                for g, part in enumerate((EH, EL)):
                    if rows:
                        row_part(*rows[:3], g, *rows[3:])
                    if part is EH:
                        pe.wait_ge(e_ready, v.now())
                    else:
                        pe.wait_ge(el_pool, v.now())
                        pe.wait_ge(el_dve, v.now())
                    for k in range(NKV):
                        ins = pe.matmul(ps[0:VW, 6 + k, :],
                                        V16[:, bass.ds(j * 2 + u, 1), k, :].rearrange("p a c -> p (a c)"),
                                        part[u][:, k * 512:(k + 1) * 512], start=first and part is EH, stop=False,
                                        skip_group_check=True)
                    if part is EH:
                        ins.then_inc(eh_used, 1)
                ins.then_inc(pv_done, 1)
                v.up()

            def through_wo(g):
                for t in range(2):
                    def fill(bank):
                        for h in range(2):
                            ins = pe.matmul(bank[:, h * (C + 1):(h + 1) * (C + 1)],
                                            OT[0:VW, g, h * BT + t * P:h * BT + (t + 1) * P],
                                            WoA[:, 2 * g + h, :], start=True, stop=True)
                        return ins
                    a_task(t, fill, z_ready)

            def diagonal_begun(i, after=True):
                second = isinstance(i, int) and i == 1
                last = 0 if second else i - 2
                chunk = 1 if second else i - 1
                pe.wait_ge(negm_done, i + 1)
                scores(i, i, 0, diagonal=True)
                values(last, 0, second, (i + 1, chunk, 0) if after else None)
                if after:
                    row_chunk(i + 1, chunk, 1)
                scores(i, i, 1, diagonal=True)
                values(last, 1, False, (i + 1, 0, 0) if after else None)
                if after:
                    row_chunk(i + 1, 0, 1)

            def attention_block(i, after=True, negate=True, inner=None):
                if after:
                    row_chunk(i + 2, i + 2, 0, diagonal=True)
                scores(i, 0, 0)
                if after:
                    row_chunk(i + 2, i + 2, 1, diagonal=True)
                if negate:
                    maxima(i + 1)
                pe.wait_ge(ot_ready, i)
                values(i, 0, True, (i + 2, i + 1, 0) if after else None)
                scores(i, 0, 1)
                through_wo(0)
                values(i, 1, False, (i + 2, i + 1, 1) if after else None)
                through_wo(1)
                if inner:
                    inner()
                elif not (isinstance(i, int) and i == 1):
                    with pe.Fori(1, i) as j:
                        for u in range(2):
                            scores(i, j, u)
                            values(j - 1, u, False, (i + 2, j, u) if after else None)
                if negate:
                    diagonal_begun(i + 1, after)

            for t in range(2):
                row_chunk(0, 0, t, diagonal=True)
            maxima(0)
            for j in (1, 0):
                for t in range(2):
                    row_chunk(1, j, t, diagonal=j == 1)
            pe.wait_ge(negm_done, 1)
            for u in range(2):
                scores(0, 0, u, diagonal=True)
            for t in range(2):
                row_chunk(2, 2, t, diagonal=True)
            maxima(1)
            diagonal_begun(1)
            attention_block(1)
            with pe.Fori(2, NB - 2) as i:
                pe.wait_ge(stacks_in[1], 16 * STACKS)
                attention_block(i)
            attention_block(NB - 2, after=False)

            def route(i):
                pe.wait_ge(turned_read, P4N + i + 1)
                wait(pe, lg_kept, i)
                for t in range(2):
                    ins = pe.matmul(ps[:, 1, t * NE:(t + 1) * NE], tb[:, t * P:(t + 1) * P], Wr,
                                    start=True, stop=True)
                ins.then_inc(lg_done, 1)

            def last_steps(j, rows_along):
                scores(NB - 1, j, 0)
                values(j - 1, 0)
                scores(NB - 1, j, 1)
                if rows_along:
                    turn(P4N + j - 2)
                values(j - 1, 1)
                if rows_along:
                    route(j - 2)

            def rows_along():
                last_steps(1, False)
                last_steps(2, True)
                with pe.Fori(3, NB - 1) as j:
                    last_steps(j, True)
            attention_block(NB - 1, after=False, negate=False, inner=rows_along)
            for u in range(2):
                values(NB - 2, u)
            for i in range(NB - 3, NB - 1):
                turn(P4N + i)
                route(i)
            pe.wait_ge(ot_ready, NB)
            pe.wait_ge(lg_kept, NB - 1)
            for g in range(NKV):
                through_wo(g)
            turn(P4N + NB - 1)
            route(NB - 1)

            pe.wait_ge(fl_done, NB)
            pe.wait_ge(fh_done, NB)
            pe.wait_ge(w_halved, 3 * NE)
            pe.wait_ge(lg_kept, NB)

            def hidden_rows(m, e, i, u):
                pe.wait_ge(gated, m + 1)
                for k, (wh, wl) in enumerate(((W1h, W1l), (W3h, W3l))):
                    for c in range(HC):
                        dst = hidden(u)[:, (k * HC + c) * BT:(k * HC + c + 1) * BT]
                        parts = ((wh, F16h), (wh, F16l), (wl, F16h))
                        for q, (wa, fa) in enumerate(parts):
                            ins = pe.matmul(dst, wa[:, e * HW + c * P:e * HW + (c + 1) * P], fa[:, bass.ts(i, BT)],
                                            start=(q == 0), stop=(q == len(parts) - 1))
                ins.then_inc(hid_done, 1)

            def expert_out(m, e, u):
                pe.wait_ge(gated_low, m + 1)
                wait(pe, acc_done, m - 1)
                for t in range(2):
                    for c in range(HC):
                        parts = ((hhh, W2h), (hhh, W2l), (hhl, W2h))
                        for q, (ha, wa) in enumerate(parts):
                            ins = pe.matmul(ps[:, 6 + u, t * C:(t + 1) * C],
                                            ha[u][:, c * BT + t * P:c * BT + (t + 1) * P],
                                            wa[:, (e * HC + c) * C:(e * HC + c + 1) * C],
                                            start=(c == 0 and q == 0), stop=(c == HC - 1 and q == len(parts) - 1))
                ins.then_inc(y_done, 1)

            def expert_turn(e2, i, nxt):
                m = e2 * (2 * NB) + i * 2
                for u in range(2):
                    if nxt:
                        hidden_rows(m + 2 + u, nxt[0] * 2 + u, nxt[1], u)
                    expert_out(m + u, e2 * 2 + u, u)

            hidden_rows(0, 0, 0, 0)
            hidden_rows(1, 1, 0, 1)
            for e2 in range(NE // 2):
                if e2 == 0:
                    expert_turn(0, 0, (0, 1))
                with pe.Fori(1 if e2 == 0 else 0, NB - 1) as i:
                    expert_turn(e2, i, (e2, i + 1))
                expert_turn(e2, NB - 1, (e2 + 1, 0) if e2 + 1 < NE // 2 else None)


def shape_tables():
    p = np.arange(P)[:, None]
    ident = np.eye(P, dtype=np.float32)
    negblk = np.zeros((P, NH, P), np.float32)
    for h in range(NH):
        negblk[h, h, :] = -1.0
    rev = np.tile(np.arange(NE, 0, -1, dtype=np.float32), (P, 1))
    tables = np.concatenate([ident, np.ones((P, P), np.float32), negblk.reshape(P, -1), rev], axis=1)
    k = np.arange(BT)[None, :]
    mask_a = np.stack([np.tile(np.where(k <= t * P + p, 0.0, FAR), (1, 2)) for t in range(2)], axis=1)
    mask_b = np.stack([np.tile(np.where(k >= t * P + p, 0.0, FAR), (1, 2)) for t in range(2)], axis=1)
    tables16 = np.concatenate([ident, mask_a.reshape(P, -1), mask_b.reshape(P, -1)], axis=1).astype(np.float16)
    inv_freq = 1.0 / 10000.0 ** (np.arange(0, HD, 2, dtype=np.float32) / HD)
    freqs = np.outer(np.arange(TP, dtype=np.float32), inv_freq)
    emb = np.concatenate([freqs, freqs], axis=-1)
    cos, sin = np.cos(emb).T, np.sin(emb).T
    sin = np.concatenate([-sin[:HD // 2], sin[HD // 2:]], axis=0)
    rope = np.stack([np.tile(cos, (P // HD, 1)), np.tile(sin, (P // HD, 1))], axis=1).astype(np.float32)
    return tables, tables16, rope


def kernel(x, adj, L0_gnn_Wq, L0_gnn_Wk, L0_ffn_ln1_w, L0_ffn_ln2_w, L0_ffn_wq, L0_ffn_wk, L0_ffn_wv,
           L0_ffn_wo, L0_ffn_router_w, L0_ffn_w1, L0_ffn_w2, L0_ffn_w3):
    import concourse.bacc as bacc
    from concourse.bass_utils import run_bass_kernel_spmd

    f = lambda v: np.asarray(v)
    tables, tables16, rope = shape_tables()
    pad = TP - NTOK
    xs = np.pad(f(x), ((0, pad), (0, 0))).reshape(NT, P, C).transpose(1, 0, 2)
    adj_t = np.pad(f(adj), ((0, pad), (0, pad))).reshape(NB, BT, NT, P).transpose(0, 3, 2, 1)

    wq, wk, wo = f(L0_ffn_wq), f(L0_ffn_wk), f(L0_ffn_wo)
    partner = lambda w: w.reshape(-1, 2, HD // 2, C)[:, ::-1].reshape(w.shape)
    to_p = lambda w: np.pad(w, ((0, P - w.shape[0]), (0, 0))).T
    wo_aug = np.zeros((P, NH, C + 1), np.float32)
    for h in range(NH):
        head = wo[:, h * HD:(h + 1) * HD].T
        wo_aug[0:HD, h, 0:C] = head
        wo_aug[HD, h, C] = 1.0
        wo_aug[HD + 1:VW, h, 0:C] = head
    w_small = np.concatenate([
        f(L0_gnn_Wq).T, f(L0_gnn_Wk).T, to_p(wq), to_p(wk), to_p(partner(wq)), to_p(partner(wk)),
        f(L0_ffn_wv).T, f(L0_ffn_router_w).T, wo_aug.reshape(P, -1),
        f(L0_ffn_ln1_w)[:, None], f(L0_ffn_ln2_w)[:, None]], axis=1)
    up = lambda w: np.pad(f(w), ((0, 0), (0, HW - HID), (0, 0))).transpose(2, 0, 1).reshape(C, NE * HW)
    down = np.pad(f(L0_ffn_w2), ((0, 0), (0, 0), (0, HW - HID))) \
        .reshape(NE, C, HC, P).transpose(3, 0, 2, 1).reshape(P, NE * HC * C)
    arrays = {"x": xs, "adj": adj_t, "w_small": w_small, "w1": up(L0_ffn_w1), "w3": up(L0_ffn_w3), "w2": down,
              "rope": rope, "tables": tables, "tables16": tables16}
    arrays = {f"in_{k}": np.ascontiguousarray(v) for k, v in arrays.items()}

    nc = bacc.Bacc("TRN2", target_bir_lowering=False, num_devices=1)
    args = [nc.dram_tensor(k, v.shape, mybir.dt.from_np(v.dtype), kind="ExternalInput").ap()
            for k, v in arrays.items()]
    args.append(nc.dram_tensor("out", (P, NT, C), F32, kind="ExternalOutput").ap())
    graph_ffn_program(nc, *args)
    r = run_bass_kernel_spmd(nc, [arrays], core_ids=[0])
    return r.results[0]["out"].transpose(1, 0, 2).reshape(TP, C)[:NTOK]
```
